# Optimizing a Trainium2 kernel written in Bass

```python
import numpy as np
import jax
import jax.numpy as jnp

def _softmax(x, axis=-1):
    return jax.nn.softmax(x, axis=axis)

def _gelu(x):
    return jax.nn.gelu(x, approximate=True)

def _silu(x):
    return jax.nn.silu(x)

def _sigmoid(x):
    return jax.nn.sigmoid(x)

def _layernorm(x, axis=-1, eps=1e-05):
    m = jnp.mean(x, axis=axis, keepdims=True)
    v = jnp.var(x, axis=axis, keepdims=True)
    return (x - m) / jnp.sqrt(v + eps)

def _scatter_add(tgt, idx, src, axis=0):
    return tgt.at[idx].add(src)

def _segment_sum(src, seg, n):
    return jax.ops.segment_sum(src, seg, n)
kernel_name = 'mk_adaln_d1_jaxref_r8_264d21'

def setup_inputs(seed: int=0):
    np.random.seed(seed)
    _w = jnp.asarray

    def _L0_attn_setup():
        import jax, jax.numpy as jnp
        import numpy as np
        D, STATE, CONV = (128, 16, 4)
        B_, L_ = (8, 256)

        def _ssm_forward(x, conv_w, conv_b, Wd, bd, Wb, Wc, log_a, Wg, bg, Wo, bo):
            b, l, d = x.shape
            xt = jnp.transpose(x, (0, 2, 1))
            xc = jax.lax.conv_general_dilated(xt, conv_w, window_strides=(1,), padding=[(CONV - 1, 0)], feature_group_count=d, dimension_numbers=('NCH', 'OIH', 'NCH'))
            xc = jnp.transpose(xc + conv_b[None, :, None], (0, 2, 1))
            xc = jax.nn.silu(xc)
            delta = jax.nn.softplus(jnp.einsum('bld,ed->ble', xc, Wd) + bd)
            Bm = jnp.einsum('bld,nd->bln', xc, Wb)
            Cm = jnp.einsum('bld,nd->bln', xc, Wc)
            A = -jnp.exp(log_a)

            def step(h, inputs):
                dt, bt, ct, xt_ = inputs
                decay = jnp.exp(A[None] * dt[:, :, None])
                inp = dt[:, :, None] * xt_[:, :, None] * bt[:, None, :]
                h = decay * h + inp
                y = jnp.einsum('bdn,bn->bd', h, ct)
                return (h, y)
            h0 = jnp.zeros((b, d, STATE), dtype=x.dtype)
            seq = (jnp.moveaxis(delta, 1, 0), jnp.moveaxis(Bm, 1, 0), jnp.moveaxis(Cm, 1, 0), jnp.moveaxis(xc, 1, 0))
            _, ys = jax.lax.scan(step, h0, seq)
            y = jnp.moveaxis(ys, 0, 1)
            gate = jax.nn.sigmoid(jnp.einsum('bld,ed->ble', x, Wg) + bg)
            return jnp.einsum('bld,ed->ble', y * gate, Wo) + bo
        key = jax.random.key(seed)
        ks = jax.random.split(key, 12)
        s = 0.02
        return {'x': jax.random.normal(ks[0], (B_, L_, D), dtype=jnp.float32), 'conv_w': jax.random.normal(ks[1], (D, 1, CONV), dtype=jnp.float32) * s, 'conv_b': jnp.zeros((D,), dtype=jnp.float32), 'Wd': jax.random.normal(ks[2], (D, D), dtype=jnp.float32) * s, 'bd': jnp.zeros((D,), dtype=jnp.float32), 'Wb': jax.random.normal(ks[3], (STATE, D), dtype=jnp.float32) * s, 'Wc': jax.random.normal(ks[4], (STATE, D), dtype=jnp.float32) * s, 'log_a': jnp.log(jnp.tile(jnp.linspace(1.0, STATE, STATE, dtype=jnp.float32), (D, 1))), 'Wg': jax.random.normal(ks[5], (D, D), dtype=jnp.float32) * s, 'bg': jnp.zeros((D,), dtype=jnp.float32), 'Wo': jax.random.normal(ks[6], (D, D), dtype=jnp.float32) * s, 'bo': jnp.zeros((D,), dtype=jnp.float32)}
    _L0_attn_in = _L0_attn_setup()

    def _L0_ffn_setup():
        import jax, jax.numpy as jnp
        import numpy as np
        NUM_EXPERTS = 8
        TOP_K = 2
        key = jax.random.key(seed)
        ks = jax.random.split(key, 5)
        B, L, E, H, N = (2, 256, 128, 256, NUM_EXPERTS)
        return {'x': jax.random.normal(ks[0], (B, L, E), dtype=jnp.float32), 'gate_kernel': jax.random.normal(ks[1], (E, N), dtype=jnp.float32) / np.sqrt(E), 'w0_kernel': jax.random.normal(ks[2], (N, E, H), dtype=jnp.float32) / np.sqrt(E), 'w1_kernel': jax.random.normal(ks[3], (N, E, H), dtype=jnp.float32) / np.sqrt(E), 'wo_kernel': jax.random.normal(ks[4], (N, H, E), dtype=jnp.float32) / np.sqrt(H)}
    _L0_ffn_in = _L0_ffn_setup()
    _L0_c = _w((lambda *s: np.random.randn(*s).astype(np.float32) * 0.05)(1, 128))
    _L0_wmod = _w((lambda *s: np.random.randn(*s).astype(np.float32) * 0.05)(128, 6 * 128) * 128 ** (-0.5))
    _d = {'L0_attn_x': _L0_attn_in['x'], 'L0_attn_conv_w': _L0_attn_in['conv_w'], 'L0_attn_conv_b': _L0_attn_in['conv_b'], 'L0_attn_Wd': _L0_attn_in['Wd'], 'L0_attn_bd': _L0_attn_in['bd'], 'L0_attn_Wb': _L0_attn_in['Wb'], 'L0_attn_Wc': _L0_attn_in['Wc'], 'L0_attn_log_a': _L0_attn_in['log_a'], 'L0_attn_Wg': _L0_attn_in['Wg'], 'L0_attn_bg': _L0_attn_in['bg'], 'L0_attn_Wo': _L0_attn_in['Wo'], 'L0_attn_bo': _L0_attn_in['bo'], 'L0_ffn_gate_kernel': _L0_ffn_in['gate_kernel'], 'L0_ffn_w0_kernel': _L0_ffn_in['w0_kernel'], 'L0_ffn_w1_kernel': _L0_ffn_in['w1_kernel'], 'L0_ffn_wo_kernel': _L0_ffn_in['wo_kernel'], 'L0_c': _L0_c, 'L0_wmod': _L0_wmod}
    _x0 = _d['L0_attn_x']
    _d['L0_attn_x'] = jax.random.normal(jax.random.fold_in(jax.random.key(seed), 1), (1, 2048, 128), dtype=_x0.dtype)
    del _x0
    return _d

def reference(L0_attn_x, L0_attn_conv_w, L0_attn_conv_b, L0_attn_Wd, L0_attn_bd, L0_attn_Wb, L0_attn_Wc, L0_attn_log_a, L0_attn_Wg, L0_attn_bg, L0_attn_Wo, L0_attn_bo, L0_ffn_gate_kernel, L0_ffn_w0_kernel, L0_ffn_w1_kernel, L0_ffn_wo_kernel, L0_c, L0_wmod):

    def _L0_attn_ref(x, conv_w, conv_b, Wd, bd, Wb, Wc, log_a, Wg, bg, Wo, bo):
        import jax, jax.numpy as jnp
        import numpy as np
        D, STATE, CONV = (128, 16, 4)
        B_, L_ = (8, 256)

        def _ssm_forward(x, conv_w, conv_b, Wd, bd, Wb, Wc, log_a, Wg, bg, Wo, bo):
            b, l, d = x.shape
            xt = jnp.transpose(x, (0, 2, 1))
            xc = jax.lax.conv_general_dilated(xt, conv_w, window_strides=(1,), padding=[(CONV - 1, 0)], feature_group_count=d, dimension_numbers=('NCH', 'OIH', 'NCH'))
            xc = jnp.transpose(xc + conv_b[None, :, None], (0, 2, 1))
            xc = jax.nn.silu(xc)
            delta = jax.nn.softplus(jnp.einsum('bld,ed->ble', xc, Wd) + bd)
            Bm = jnp.einsum('bld,nd->bln', xc, Wb)
            Cm = jnp.einsum('bld,nd->bln', xc, Wc)
            A = -jnp.exp(log_a)

            def step(h, inputs):
                dt, bt, ct, xt_ = inputs
                decay = jnp.exp(A[None] * dt[:, :, None])
                inp = dt[:, :, None] * xt_[:, :, None] * bt[:, None, :]
                h = decay * h + inp
                y = jnp.einsum('bdn,bn->bd', h, ct)
                return (h, y)
            h0 = jnp.zeros((b, d, STATE), dtype=x.dtype)
            seq = (jnp.moveaxis(delta, 1, 0), jnp.moveaxis(Bm, 1, 0), jnp.moveaxis(Cm, 1, 0), jnp.moveaxis(xc, 1, 0))
            _, ys = jax.lax.scan(step, h0, seq)
            y = jnp.moveaxis(ys, 0, 1)
            gate = jax.nn.sigmoid(jnp.einsum('bld,ed->ble', x, Wg) + bg)
            return jnp.einsum('bld,ed->ble', y * gate, Wo) + bo
        return _ssm_forward(x, conv_w, conv_b, Wd, bd, Wb, Wc, log_a, Wg, bg, Wo, bo)

    def _L0_ffn_ref(x, gate_kernel, w0_kernel, w1_kernel, wo_kernel):
        import jax, jax.numpy as jnp
        import numpy as np
        NUM_EXPERTS = 8
        TOP_K = 2
        B, L, E = x.shape
        gate_logits = jnp.einsum('ble,en->bln', x, gate_kernel)
        top_k_weights, top_k_indices = jax.lax.top_k(gate_logits, TOP_K)
        softmax_probs = jax.nn.softmax(top_k_weights.astype(jnp.float32), axis=-1)
        weights = jnp.zeros_like(gate_logits)
        b_idx = jnp.arange(B)[:, None, None]
        l_idx = jnp.arange(L)[:, None]
        weights = weights.at[b_idx, l_idx, top_k_indices].set(softmax_probs)
        layer_w0 = jnp.einsum('ble,neh->blnh', x, w0_kernel)
        layer_w1 = jnp.einsum('ble,neh->blnh', x, w1_kernel)
        layer_mult = jax.nn.silu(layer_w0) * layer_w1
        intermediate = jnp.einsum('blnh,nhe->blne', layer_mult, wo_kernel)
        output = jnp.einsum('blne,bln->ble', intermediate, weights)
        return output
    x = L0_attn_x
    mod = (_silu(L0_c) @ L0_wmod).reshape(L0_c.shape[0], 6, 1, -1)
    sa, ca, ga, sb, cb, gb = (mod[:, 0], mod[:, 1], mod[:, 2], mod[:, 3], mod[:, 4], mod[:, 5])
    ga = (2 * (ga >= 0) - 1) * jnp.maximum(jnp.abs(ga), 0.25)
    gb = (2 * (gb >= 0) - 1) * jnp.maximum(jnp.abs(gb), 0.25)
    h = _layernorm(x, axis=-1) * (1 + ca) + sa
    x = x + ga * _L0_attn_ref(h, L0_attn_conv_w, L0_attn_conv_b, L0_attn_Wd, L0_attn_bd, L0_attn_Wb, L0_attn_Wc, L0_attn_log_a, L0_attn_Wg, L0_attn_bg, L0_attn_Wo, L0_attn_bo)
    h = _layernorm(x, axis=-1) * (1 + cb) + sb
    x = x + gb * _L0_ffn_ref(h, L0_ffn_gate_kernel, L0_ffn_w0_kernel, L0_ffn_w1_kernel, L0_ffn_wo_kernel)
    return x

_drawn_inputs = setup_inputs


def setup_inputs(seed=0):
    import zlib

    import numpy as np

    out = dict(_drawn_inputs(seed))
    spreads = {'L0_attn_conv_b': (0.0, 0.8),
     'L0_attn_bd': (0.0, 0.8),
     'L0_attn_bg': (0.0, 0.8),
     'L0_attn_bo': (0.0, 0.278)}
    factors = {'L0_attn_conv_w': 8.0,
     'L0_attn_Wd': 8.0,
     'L0_attn_Wb': 8.0,
     'L0_attn_Wc': 8.0,
     'L0_attn_log_a': 8.0,
     'L0_attn_Wg': 8.0,
     'L0_attn_Wo': 8.0}
    for name, (base, spread) in spreads.items():
        noise = np.random.default_rng([zlib.crc32(name.encode()), seed]).standard_normal(out[name].shape)
        drawn = base * np.exp(spread * noise) if base else spread * noise
        out[name] = jnp.asarray(drawn.astype(out[name].dtype))
    for name, factor in factors.items():
        out[name] = (out[name] * factor).astype(out[name].dtype)
    return out
```

```python
from contextlib import ExitStack

import concourse.bass as bass
from concourse import mybir

ALU = mybir.AluOpType
ACT = mybir.ActivationFunctionType
F32 = mybir.dt.float32
F32R = mybir.dt.float32r
U32 = mybir.dt.uint32

P = 128
TC = 512
JT = TC // P
D = 128
NS = 16
GC = P // NS
NG = D // GC
NE = 8
H = 256
NH = NE * H // P
HE = H // P
TAPS = 4
PAD = TAPS - 1
EPS = 1e-5
GATE_MIN = 0.25
ND = 12
QB = 4

C_CONVW, C_CONVB, C_BD, C_BG, C_BO, C_C = 0, 4, 5, 6, 7, 8
C_ROUTE, C_LOGA, C_WB, C_WC = 9, 17, 33, 49
N_SMALL = 65
M_WD, M_WG, M_WO, M_MOD = 0, 128, 256, 384
N_DENSE = 384 + 6 * 128
K_ID, K_FOLD, K_SUM, K_EXP, K_IOTA = 0, 128, 192, 320, 328
N_CONST = 336

GROUPS = [(k % QB) * (NG // QB) + k // QB for k in range(NG)]


def schedule():
    order = []
    ups = scans = downs = sums = 0

    def scan():
        nonlocal scans, sums
        order.append(("scan", scans))
        scans += 1
        if scans % QB == 2 and scans > QB:
            order.append(("sum", sums))
            sums += 1

    def up():
        nonlocal ups, downs
        order.append(("up", ups))
        ups += 1
        if ups > 2:
            order.append(("down", downs))
            downs += 1

    order.append(("decay", 0))
    for k in range(1, NG):
        order.append(("decay", k))
        if k % 2 == 1:
            scan()
    while ups < NH or scans < NG:
        if ups < NH:
            up()
        if ups < NH:
            up()
        if scans < NG:
            scan()
    while downs < NH:
        order.append(("down", downs))
        downs += 1
    while sums < NG // QB:
        order.append(("sum", sums))
        sums += 1
    return order


ORDER = schedule()


def program(nc, x_in, small_in, dense_in, const_in, w0_in, w1_in, wo_in, out):
    tokens = x_in.shape[1] * P // D
    NC = tokens // TC

    with ExitStack() as ctx:
        def sb(name, shape, dt=F32):
            return ctx.enter_context(nc.sbuf_tensor(name, shape, dt))

        def sem(name):
            return ctx.enter_context(nc.semaphore(name))

        x = sb("x", [P, NC * TC])
        small = sb("small", [P, N_SMALL])
        dense = sb("dense", [P, N_DENSE])
        const = sb("const", [P, N_CONST])
        hT = sb("hT", [P, PAD + NC * TC])
        xcT = sb("xcT", [P, NC * TC])
        gateT = sb("gateT", [P, NC * TC])
        decay = sb("decay", [P, ND, TC])
        w_raw = decay[:, 0:8, :].rearrange("p a t -> p (a t)")
        w0_hi = sb("w0_hi", [P, NE * H], F32R)
        w0_lo = sb("w0_lo", [P, NE * H], F32R)
        w1_hi = sb("w1_hi", [P, NE * H], F32R)
        w1_lo = sb("w1_lo", [P, NE * H], F32R)
        wo = sb("wo", [P, NH, D])
        pick = sb("pick", [P, 8, P], F32R)
        expert_pick = sb("expert_pick", [2 * NE, NE, P], F32R)
        wb_rep = sb("wb_rep", [P, P])
        wc_rep = sb("wc_rep", [P, P])
        wo_g = sb("wo_g", [P, P])
        wo_gT = sb("wo_gT", [P, P])
        bo_row = sb("bo_row", [1, P])
        ones = sb("ones", [1, P])
        cvec = sb("cvec", [P, 32])
        neg_a = sb("neg_a", [P, NG])
        state = sb("state", [P, NG])
        stats = sb("stats", [P, NC * JT, 6])
        mv = sb("mv", [P, NC * JT, 2])
        mv2 = sb("mv2", [P, JT, 2])
        veps = sb("veps", [P, NC * JT])
        veps2 = sb("veps2", [P, JT])
        rstd = sb("rstd", [P, NC * JT])
        rstd2 = sb("rstd2", [P, JT])
        mhalf = sb("mhalf", [P, NC * JT])
        xn = sb("xn", [P, JT, P])
        zz = sb("zz", [P, 3, TC])
        z, za, ze = zz[:, 0, :], zz[:, 1, :], zz[:, 2, :]
        acc, th = zz[:, 0:2, :], zz[:, 2, :]
        zu = sb("zu", [P, TC])
        zl = sb("zl", [P, TC])
        delta = sb("delta", [P, TC])
        dx = sb("dx", [P, TC])
        delta_r = sb("delta_r", [P, 2, TC], F32R)
        dx_r = sb("dx_r", [P, 2, TC], F32R)
        bb = sb("bb", [P, TC])
        cb = sb("cb", [P, TC])
        h = sb("h", [P, QB, TC])
        hc = sb("hc", [P, 2 * QB, TC])
        yg = sb("yg", [P, TC])
        h2 = sb("h2", [P, TC])
        h2_hi = sb("h2_hi", [P, TC], F32R)
        h2_lo = sb("h2_lo", [P, TC], F32R)
        lg = sb("lg", [P, JT, NE])
        top = sb("top", [P, JT, 8])
        topi = sb("topi", [P, JT, 8], U32)
        gt = sb("gt", [P, 8, JT, NE])
        wr = sb("wr", [P, JT, 2 * NE])
        wr_hi = sb("wr_hi", [P, JT, NE], F32R)
        wrT = sb("wrT", [2 * NE, TC], F32R)
        wbc = sb("wbc", [P, NE, TC])
        act_u = hT[:, 0:2 * TC].rearrange("p (a t) -> p a t", a=2)
        mul_u = hT[:, 2 * TC:4 * TC].rearrange("p (a t) -> p a t", a=2)
        mw = sb("mw", [P, 4, TC])
        fo = zl
        res = sb("res", [P, TC])

        def bank(name):
            return ctx.enter_context(nc.psum_tensor(name, [P, TC], F32))

        p_dec = [bank("p_dec0"), bank("p_dec1")]
        p_inp = [bank("p_inp0"), bank("p_inp1")]
        p_y = bank("p_y")
        p_up = [bank("p_up0"), bank("p_up1")]
        p_out = bank("p_out")

        ident = const[:, K_ID:K_ID + P]
        wdT = dense[:, M_WD:M_WD + P]
        wgT = dense[:, M_WG:M_WG + P]
        wo_attn = dense[:, M_WO:M_WO + P]
        sa, one_ca, sb_, one_cb = (cvec[:, i:i + 1] for i in range(4))
        ga, gb = cvec[:, 4:5], cvec[:, 5:6]
        half_bg = cvec[:, 20:21]
        silu_c = cvec[:, 21:22]
        bo_g = cvec[:, 22:23]

        names = """const_in small_in dense_in x_in w_in wo_in
            dve_set act_set pe_set pool_set w_hi w_lo mod_ready
            stat1 aggr1 eps1 rstd1 xn1 xn1_t h_ready conv_step acc_ready xc_ready
            gatez_ready th_ready gate_ready
            z_ready b_ready c_ready zb za ze zu zl zt delta_ready d_hi d_lo dx_done dx_hi dx_lo bb_ready cb_ready
            dec_ready decayed inp_ready mixed scanned carried hc_ready summed yg_ready
            attn_ready x2_ready stat2 aggr2 eps2 rstd2_ready xn2 xn2_t h2_ready h2_hi_ready h2_lo_ready
            lg_ready lg_copied top_ready topi_ready route_diff route_exp route_step wr_ready wrT_ready wrT_copied
            wbc_ready wbc_copied gate_up lin_up silued multiplied weighted down_done
            fo_ready foT_ready res_ready out_done""".split()
        s = {n: sem("s_" + n) for n in names}

        def wait(eng, name, c, per, k):
            if k < 0:
                return
            v = c * per + k
            if not isinstance(v, int) or v > 0:
                eng.wait_ge(s[name], v)

        def chunk(t, c, off=0, n=TC):
            if isinstance(c, int):
                return t[:, c * TC + off:c * TC + off + n]
            return t[:, bass.ds(c * TC + off, n)]

        block = ctx.enter_context(nc.Block())

        @block.sync
        def _(sp):
            sp.dma_start(small[:], small_in).then_inc(s["small_in"], 16)
            sp.dma_start(x[:], x_in).then_inc(s["x_in"], 16)
            sp.dma_start(const[:], const_in).then_inc(s["const_in"], 16)
            sp.dma_start(dense[:], dense_in).then_inc(s["dense_in"], 16)
            sp.dma_start(w_raw[:, 0:NE * H], w0_in).then_inc(s["w_in"], 16)
            sp.dma_start(w_raw[:, NE * H:2 * NE * H], w1_in).then_inc(s["w_in"], 16)
            sp.dma_start(wo[:].rearrange("p a e -> p (a e)"), wo_in).then_inc(s["wo_in"], 16)

            def store(c):
                wait(sp, "res_ready", c, 1, 2)
                src = res[:]
                sp.dma_start(chunk(out, c), src).then_inc(s["out_done"], 16)

            with sp.Fori(0, NC) as c:
                store(c)
            sp.wait_ge(s["out_done"], 16 * (NC + 1))

        @block.scalar
        def _(act):
            act.wait_ge(s["small_in"], 16)
            nc.scalar.activation(silu_c, small[:, C_C:C_C + 1], ACT.Silu).then_inc(s["act_set"], 1)
            nc.scalar.activation(neg_a[:], small[:, C_LOGA:C_LOGA + NG], ACT.Exp).then_inc(s["act_set"], 1)
            act.wait_ge(s["act_set"], 2)
            nc.scalar.mul(neg_a[:], neg_a[:], -1.0).then_inc(s["act_set"], 1)
            act.wait_ge(s["w_in"], 32)
            nc.scalar.copy(w0_hi[:], w_raw[:, 0:NE * H]).then_inc(s["w_hi"], 1)
            nc.scalar.copy(w1_hi[:], w_raw[:, NE * H:2 * NE * H]).then_inc(s["w_hi"], 1)
            act.wait_ge(s["mod_ready"], 1)

            def prepare(c):
                wait(act, "xn1_t", c, 1, 1)
                nc.scalar.activation(chunk(hT, c, PAD), p_dec[0][:], ACT.Identity, bias=sa,
                                     scale=one_ca).then_inc(s["h_ready"], 1)
                wait(act, "gatez_ready", c, 1, 1)
                nc.scalar.activation(th, p_dec[1][:], ACT.Tanh, bias=half_bg,
                                     scale=0.5).then_inc(s["th_ready"], 1)
                wait(act, "acc_ready", c, 1, 1)
                nc.scalar.activation(chunk(xcT, c), acc[:, 0, :], ACT.Silu,
                                     bias=small[:, C_CONVB:C_CONVB + 1]).then_inc(s["xc_ready"], 1)
                wait(act, "gate_ready", c, 1, 1)

            prepare(0)
            with act.Fori(1, NC) as c:
                prepare(c)

            def step(c, scan, ffn):
                f = c - 1
                if scan:
                    wait(act, "b_ready", c, 1, 1)
                    wait(act, "mixed", c, NG, 0)
                    nc.scalar.copy(bb[:], p_inp[1][:]).then_inc(s["bb_ready"], 1)
                    wait(act, "c_ready", c, 1, 1)
                    wait(act, "hc_ready", c, NG, 0)
                    nc.scalar.copy(cb[:], p_dec[1][:]).then_inc(s["cb_ready"], 1)
                    wait(act, "za", c, 1, 1)
                    nc.scalar.activation(ze, za, ACT.Exp, scale=-1.0).then_inc(s["ze"], 1)
                    wait(act, "zu", c, 1, 1)
                    nc.scalar.activation(zl[:], zu[:], ACT.Ln).then_inc(s["zl"], 1)
                    wait(act, "delta_ready", c, 1, 1)
                    nc.scalar.copy(delta_r[0:64, 0, :], delta[0:64, :]).then_inc(s["d_hi"], 1)
                    nc.scalar.copy(delta_r[64:128, 1, :], delta[64:128, :]).then_inc(s["d_hi"], 1)
                    wait(act, "dx_done", c, 1, 1)
                    wait(act, "inp_ready", c, NG, 0)
                    nc.scalar.copy(dx_r[0:64, 0, :], dx[0:64, :]).then_inc(s["dx_hi"], 1)
                    nc.scalar.copy(dx_r[64:128, 1, :], dx[64:128, :]).then_inc(s["dx_hi"], 1)
                if ffn:
                    wait(act, "xn2_t", f, 1, 1)
                    nc.scalar.activation(h2[:], p_up[1][:], ACT.Identity, bias=sb_,
                                         scale=one_cb).then_inc(s["h2_ready"], 1)
                    wait(act, "h2_ready", f, 1, 1)
                    nc.scalar.copy(h2_hi[:], h2[:]).then_inc(s["h2_hi_ready"], 1)
                    wait(act, "route_diff", f, 1, 1)
                    nc.scalar.activation(gt[:, 0, :, 1:2], gt[:, 0, :, 0:1], ACT.Exp,
                                         scale=-1.0).then_inc(s["route_exp"], 1)
                    wait(act, "wrT_ready", f, 1, 1)
                    nc.scalar.copy(wrT[:], p_up[0][0:2 * NE, :]).then_inc(s["wrT_copied"], 1)
                    for n in range(NE):
                        wait(act, "wbc_ready", f, NE, n + 1)
                        nc.scalar.copy(wbc[:, n, :], p_up[(n + 1) % 2][:]).then_inc(s["wbc_copied"], 1)
                for kind, k in ORDER:
                    if kind == "decay" and scan:
                        wait(act, "dec_ready", c, NG, k + 1)
                        wait(act, "scanned", c, NG, k + 1 - ND)
                        nc.scalar.activation(decay[:, k % ND, :], p_dec[k % 2][:], ACT.Exp,
                                             scale=neg_a[:, GROUPS[k]:GROUPS[k] + 1]).then_inc(s["decayed"], 1)
                    if kind == "up" and ffn:
                        wait(act, "gate_up", f, NH, k + 1)
                        wait(act, "multiplied", f, NH, k - 1)
                        nc.scalar.activation(act_u[:, k % 2, :], p_up[0][:], ACT.Silu).then_inc(s["silued"], 1)
                if ffn:
                    wait(act, "down_done", f, NH, NH)
                    nc.scalar.activation(fo[:], p_out[:], ACT.Identity, scale=gb).then_inc(s["fo_ready"], 1)

            act.wait_ge(s["w_lo"], 2)
            step(0, True, False)
            with act.Fori(1, NC) as c:
                step(c, True, True)
            step(NC, False, True)

        @block.vector
        def _(dve):
            n_set = 0

            def setup(ins):
                nonlocal n_set
                n_set += 1
                ins.then_inc(s["dve_set"], 1)

            def settle():
                dve.wait_ge(s["dve_set"], n_set)

            dve.nop().then_inc(s["res_ready"], 1)
            dve.nop().then_inc(s["out_done"], 16)
            setup(dve.memset(state[:], 0.0))
            setup(dve.memset(hT[:, 0:PAD], 0.0))
            setup(dve.memset(ones[:], 1.0))
            dve.wait_ge(s["small_in"], 16)
            setup(dve.tensor_scalar(half_bg, small[:, C_BG:C_BG + 1], 0.5, None, ALU.mult))
            for rep, col in ((wb_rep, C_WB), (wc_rep, C_WC)):
                src = small[:, col:col + NS].rearrange("p (n i) -> p n i", i=1).to_broadcast([P, NS, GC])
                setup(dve.tensor_copy(rep[:].rearrange("p (n i) -> p n i", i=GC), src))

            dve.wait_ge(s["x_in"], 16)
            for m in range(NC * JT):
                dve.bn_stats(stats[:, m, :], x[:, m * P:(m + 1) * P]).then_inc(s["stat1"], 1)
            for m in range(NC * JT):
                dve.wait_ge(s["stat1"], m + 1)
                dve.bn_aggr(mv[:, m, :], stats[:, m, :]).then_inc(s["aggr1"], 1)
            dve.wait_ge(s["aggr1"], NC * JT)
            dve.tensor_scalar(veps[:], mv[:, :, 1], EPS, None, ALU.add).then_inc(s["eps1"], 1)

            dve.wait_ge(s["const_in"], 16)
            for g in range(8):
                src = const[:, K_FOLD + g * GC:K_FOLD + (g + 1) * GC].rearrange(
                    "p (n i) -> p n i", n=1).to_broadcast([P, NS, GC])
                setup(dve.tensor_copy(pick[:, g, :].rearrange("p (n i) -> p n i", i=GC), src))
            setup(dve.tensor_copy(expert_pick[:], const[0:2 * NE, K_EXP:K_EXP + NE].rearrange(
                "p (n i) -> p n i", i=1).to_broadcast([2 * NE, NE, P])))

            dve.wait_ge(s["pe_set"], 1)
            setup(dve.tensor_copy(cvec[:, 0:6], p_out[:, 0:6]))
            settle()
            setup(dve.tensor_scalar(cvec[:, 1:4:2], cvec[:, 1:4:2], 1.0, None, ALU.add))
            setup(dve.tensor_scalar(cvec[:, 8:10], cvec[:, 4:6], 0.0, 2.0, ALU.is_ge, ALU.mult))
            setup(dve.scalar_tensor_tensor(cvec[:, 10:12], cvec[:, 4:6], -1.0, cvec[:, 4:6], ALU.mult, ALU.max))
            settle()
            setup(dve.tensor_scalar(cvec[:, 12:14], cvec[:, 10:12], GATE_MIN, None, ALU.max))
            settle()
            setup(dve.scalar_tensor_tensor(cvec[:, 4:6], cvec[:, 8:10], -1.0, cvec[:, 12:14], ALU.add, ALU.mult))
            settle()
            setup(dve.tensor_scalar(wo_g[:], wo_attn, ga, None, ALU.mult))
            setup(dve.tensor_scalar(bo_g, small[:, C_BO:C_BO + 1], ga, None, ALU.mult))
            settle()
            dve.nop().then_inc(s["mod_ready"], 1)
            dve.wait_ge(s["pe_set"], 2)
            setup(dve.tensor_copy(wo_gT[:], p_y[:, 0:P]))
            setup(dve.tensor_copy(bo_row[:], p_y[0:1, P:2 * P]))

            dve.wait_ge(s["rstd1"], 1)
            def prepare(c):
                wait(dve, "xn1_t", c, 1, 0)
                for j in range(JT):
                    m = bass.ds(c * JT + j, 1)
                    dve.tensor_scalar(xn[:, j, :], chunk(x, c, j * P, P),
                                      mv[:, m, 0], rstd[:, m],
                                      ALU.subtract, ALU.mult).then_inc(s["xn1"], 1)
                wait(dve, "h_ready", c, 1, 1)
                dve.tensor_scalar(acc[:, 0, :], chunk(hT, c), small[:, C_CONVW:C_CONVW + 1], None,
                                  ALU.mult).then_inc(s["conv_step"], 1)
                for k in range(1, TAPS):
                    wait(dve, "conv_step", c, TAPS - 1, k)
                    dve.scalar_tensor_tensor(acc[:, (k + 0) % 2, :] if k < TAPS - 1 else acc[:, 0, :],
                                             chunk(hT, c, k), small[:, C_CONVW + k:C_CONVW + k + 1],
                                             acc[:, (k + 1) % 2, :] if k < TAPS - 1 else acc[:, 0, :],
                                             ALU.mult, ALU.add).then_inc(
                        s["conv_step"] if k < TAPS - 1 else s["acc_ready"], 1)
                wait(dve, "th_ready", c, 1, 1)
                dve.tensor_scalar(chunk(gateT, c), th, 0.5, 0.5, ALU.mult, ALU.add).then_inc(s["gate_ready"], 1)

            prepare(0)
            with dve.Fori(1, NC) as c:
                prepare(c)

            def hold(name, c, per, k):
                wait(dve, name, c, per, k)
                dve.tensor_copy(cvec[:, 30:31], cvec[:, 0:1])

            def step(c, scan, ffn):
                f = c - 1
                if scan:
                    wait(dve, "z_ready", c, 1, 1)
                    dve.tensor_scalar(z, p_inp[0][:], small[:, C_BD:C_BD + 1], None,
                                      ALU.add).then_inc(s["zb"], 1)
                    wait(dve, "zb", c, 1, 1)
                    dve.scalar_tensor_tensor(za, z, -1.0, z, ALU.mult, ALU.max).then_inc(s["za"], 1)
                if ffn:
                    wait(dve, "attn_ready", f, 1, 1)
                    dve.tensor_tensor(chunk(x, f), chunk(x, f), p_up[0][:], ALU.add).then_inc(s["x2_ready"], 1)
                    hold("x2_ready", f, 1, 1)
                    for j in range(JT):
                        dve.bn_stats(stats[:, j, :], chunk(x, f, j * P, P)).then_inc(s["stat2"], 1)
                    hold("stat2", f, JT, JT)
                    for j in range(JT):
                        dve.bn_aggr(mv2[:, j, :], stats[:, j, :]).then_inc(s["aggr2"], 1)
                    wait(dve, "aggr2", f, JT, JT)
                    dve.tensor_scalar(veps2[:], mv2[:, :, 1], EPS, None, ALU.add).then_inc(s["eps2"], 1)
                if scan:
                    wait(dve, "ze", c, 1, 1)
                    dve.tensor_scalar(zu[:], ze, 1.0, None, ALU.add).then_inc(s["zu"], 1)
                    wait(dve, "zu", c, 1, 1)
                    dve.scalar_tensor_tensor(za, zu[:], -1.0, ze, ALU.add, ALU.subtract).then_inc(s["zt"], 1)
                    wait(dve, "zt", c, 2, 1)
                    dve.scalar_tensor_tensor(z, z, 0.0, za, ALU.max, ALU.subtract).then_inc(s["zt"], 1)
                if ffn:
                    wait(dve, "rstd2_ready", f, 1, 1)
                    for j in range(JT):
                        dve.tensor_scalar(xn[:, j, :], chunk(x, f, j * P, P), mv2[:, j, 0:1], rstd2[:, j:j + 1],
                                          ALU.subtract, ALU.mult).then_inc(s["xn2"], 1)
                if scan:
                    wait(dve, "zl", c, 1, 1)
                    wait(dve, "zt", c, 2, 2)
                    dve.tensor_tensor(delta[:], z, zl[:], ALU.add).then_inc(s["delta_ready"], 1)
                    wait(dve, "delta_ready", c, 1, 1)
                    dve.tensor_tensor(dx[:], delta[:], chunk(xcT, c), ALU.mult).then_inc(s["dx_done"], 1)
                    for name, full, parts, hi in (("d_lo", delta, delta_r, "d_hi"), ("dx_lo", dx, dx_r, "dx_hi")):
                        wait(dve, hi, c, 2, 1)
                        dve.tensor_tensor(parts[64:128, 0, :], full[0:64, :], parts[0:64, 0, :].bitcast(F32),
                                          ALU.subtract).then_inc(s[name], 1)
                        wait(dve, hi, c, 2, 2)
                        dve.tensor_tensor(parts[0:64, 1, :], full[64:128, :], parts[64:128, 1, :].bitcast(F32),
                                          ALU.subtract).then_inc(s[name], 1)
                if ffn:
                    wait(dve, "h2_hi_ready", f, 1, 1)
                    dve.tensor_tensor(h2_lo[:], h2[:], h2_hi[:].bitcast(F32), ALU.subtract).then_inc(s["h2_lo_ready"], 1)
                    wait(dve, "lg_ready", f, 1, 1)
                    dve.tensor_copy(lg[:], p_up[0][:, 0:JT * NE].rearrange("p (j n) -> p j n", n=NE)
                                    ).then_inc(s["lg_copied"], 1)
                    hold("lg_copied", f, 1, 1)
                    for j in range(JT):
                        dve.max(top[:, j, :], lg[:, j, :]).then_inc(s["top_ready"], 1)
                    wait(dve, "top_ready", f, JT, JT)
                    dve.tensor_tensor(gt[:, 0, :, 0:1], top[:, :, 0:1], top[:, :, 1:2],
                                      ALU.subtract).then_inc(s["route_diff"], 1)
                    for j in range(JT):
                        dve.max_index(topi[:, j, :], top[:, j, :], lg[:, j, :]).then_inc(s["topi_ready"], 1)
                    wait(dve, "topi_ready", f, JT, JT)
                    R = 9
                    r = 0

                    def link(ins):
                        nonlocal r
                        r += 1
                        ins.then_inc(s["route_step"], 1)
                        wait(dve, "route_step", f, R, r)

                    link(dve.tensor_copy(gt[:, 1, :, 0:2], topi[:, :, 0:2]))
                    iota = const[:, K_IOTA:K_IOTA + NE].rearrange("p (j n) -> p j n", j=1).to_broadcast([P, JT, NE])
                    for i in range(2):
                        link(dve.tensor_tensor(gt[:, 2 + i], iota, gt[:, 1, :, i:i + 1].to_broadcast([P, JT, NE]),
                                               ALU.is_equal))
                    wait(dve, "route_exp", f, 1, 1)
                    link(dve.tensor_scalar(gt[:, 0, :, 2:3], gt[:, 0, :, 1:2], 1.0, None, ALU.add))
                    link(dve.reciprocal(gt[:, 0, :, 3:4], gt[:, 0, :, 2:3]))
                    link(dve.tensor_tensor(gt[:, 0, :, 4:5], gt[:, 0, :, 1:2], gt[:, 0, :, 3:4], ALU.mult))
                    for i in range(2):
                        link(dve.tensor_tensor(gt[:, 4 + i], gt[:, 2 + i],
                                               gt[:, 0, :, 3 + i:4 + i].to_broadcast([P, JT, NE]), ALU.mult))
                    link(dve.tensor_tensor(gt[:, 6], gt[:, 4], gt[:, 5], ALU.add))
                    dve.tensor_copy(wr_hi[:], gt[:, 6]).then_inc(s["wr_ready"], 1)
                    wait(dve, "wr_ready", f, 3, 1)
                    dve.tensor_copy(wr[:, :, 0:NE], wr_hi[:].bitcast(F32)).then_inc(s["wr_ready"], 1)
                    dve.tensor_tensor(wr[:, :, NE:2 * NE], gt[:, 6], wr_hi[:].bitcast(F32),
                                      ALU.subtract).then_inc(s["wr_ready"], 1)
                for kind, k in ORDER:
                    if kind == "scan" and scan:
                        wait(dve, "inp_ready", c, NG, k + 1)
                        wait(dve, "bb_ready", c, 1, 1)
                        dve.tensor_tensor(p_inp[k % 2][:], p_inp[k % 2][:], bb[:], ALU.mult).then_inc(s["mixed"], 1)
                        wait(dve, "mixed", c, NG, k + 1)
                        wait(dve, "decayed", c, NG, k + 1)
                        wait(dve, "carried", c, NG, 0)
                        wait(dve, "hc_ready", c, NG, k - QB + 1)
                        dve.tensor_tensor_scan(h[:, k % QB, :], decay[:, k % ND, :], p_inp[k % 2][:], state[:, k:k + 1],
                                               ALU.mult, ALU.add).then_inc(s["scanned"], 1)
                        wait(dve, "scanned", c, NG, k + 1)
                        dve.tensor_copy(state[:, k:k + 1], h[:, k % QB, TC - 1:TC]).then_inc(s["carried"], 1)
                    if kind == "up" and ffn:
                        wait(dve, "lin_up", f, NH, k + 1)
                        wait(dve, "silued", f, NH, k + 1)
                        wait(dve, "weighted", f, NH, k - 1)
                        dve.tensor_tensor(mul_u[:, k % 2, :], act_u[:, k % 2, :], p_up[1][:],
                                          ALU.mult).then_inc(s["multiplied"], 1)
                if scan:
                    wait(dve, "summed", c, NG // QB, NG // QB)
                    dve.tensor_tensor(yg[:], p_y[:], chunk(gateT, c), ALU.mult).then_inc(s["yg_ready"], 1)
                if ffn:
                    wait(dve, "foT_ready", f, 1, 1)
                    wait(dve, "out_done", f, 16, 16)
                    dve.tensor_tensor(res[:], chunk(x, f), p_up[0][:], ALU.add).then_inc(s["res_ready"], 1)

            step(0, True, False)
            with dve.Fori(1, NC) as c:
                step(c, True, True)
            step(NC, False, True)

        @block.gpsimd
        def _(pool):
            pool.memset(mhalf[:], -0.5).then_inc(s["pool_set"], 1)
            pool.wait_ge(s["eps1"], 1)
            pool.wait_ge(s["pool_set"], 1)
            pool.tensor_tensor(rstd[:], veps[:], mhalf[:], ALU.pow).then_inc(s["rstd1"], 1)
            for i, (hi, lo) in enumerate(((w0_hi, w0_lo), (w1_hi, w1_lo))):
                pool.wait_ge(s["w_hi"], i + 1)
                pool.tensor_tensor(lo[:], w_raw[:, i * NE * H:(i + 1) * NE * H], hi[:].bitcast(F32),
                                   ALU.subtract).then_inc(s["w_lo"], 1)

            def step(c, scan, ffn):
                f = c - 1
                if ffn:
                    wait(pool, "eps2", f, 1, 1)
                    pool.tensor_tensor(rstd2[:], veps2[:], mhalf[:, 0:JT], ALU.pow).then_inc(s["rstd2_ready"], 1)
                for kind, k in ORDER:
                    if kind == "scan" and scan:
                        wait(pool, "scanned", c, NG, k + 1)
                        wait(pool, "cb_ready", c, 1, 1)
                        wait(pool, "summed", c, NG // QB, k // QB - 1)
                        pool.tensor_tensor(hc[:, k % (2 * QB), :], h[:, k % QB, :], cb[:],
                                           ALU.mult).then_inc(s["hc_ready"], 1)
                    if kind == "up" and ffn:
                        wait(pool, "multiplied", f, NH, k + 1)
                        wait(pool, "wbc_copied", f, NE, NE)
                        wait(pool, "down_done", f, NH, k - 3)
                        pool.tensor_tensor(mw[:, k % 4, :], mul_u[:, k % 2, :], wbc[:, k // HE, :],
                                           ALU.mult).then_inc(s["weighted"], 1)

            step(0, True, False)
            with pool.Fori(1, NC) as c:
                step(c, True, True)
            step(NC, False, True)

        @block.tensor
        def _(pe):
            pe.wait_ge(s["dense_in"], 16)
            pe.wait_ge(s["act_set"], 1)
            for col, part in enumerate((0, 1, 3, 4, 2, 5)):
                ins = pe.matmul(p_out[:, col:col + 1], dense[:, M_MOD + part * D:M_MOD + (part + 1) * D], silu_c,
                                start=True, stop=True)
            ins.then_inc(s["pe_set"], 1)
            pe.wait_ge(s["mod_ready"], 1)
            pe.transpose(p_y[:, 0:P], wo_g[:], ident)
            pe.matmul(p_y[0:1, P:2 * P], bo_g, ident, start=True, stop=True).then_inc(s["pe_set"], 1)

            def prepare(c):
                wait(pe, "h_ready", c, 1, 0)
                wait(pe, "xn1", c, JT, JT)
                for j in range(JT):
                    ins = pe.transpose(p_dec[0][:, j * P:(j + 1) * P], xn[:, j, :], ident)
                ins.then_inc(s["xn1_t"], 1)
                wait(pe, "th_ready", c, 1, 0)
                wait(pe, "h_ready", c, 1, 1)
                pe.matmul(p_dec[1][:], wgT, chunk(hT, c, PAD), start=True, stop=True).then_inc(s["gatez_ready"], 1)

            prepare(0)
            with pe.Fori(1, NC) as c:
                prepare(c)

            def split_product(out_bank, hi, lo, q, done):
                cols = slice(q * P, (q + 1) * P)
                pe.matmul(out_bank[:], hi[:, cols], h2_hi[:], start=True, stop=False)
                pe.matmul(out_bank[:], hi[:, cols], h2_lo[:], start=False, stop=False)
                pe.matmul(out_bank[:], lo[:, cols], h2_hi[:], start=False, stop=True).then_inc(s[done], 1)

            def step(c, scan, ffn):
                f = c - 1
                if scan:
                    wait(pe, "xc_ready", c, 0, NC)
                    wait(pe, "scanned", c, NG, 0)
                    pe.matmul(p_inp[0][:], wdT, chunk(xcT, c), start=True, stop=True).then_inc(s["z_ready"], 1)
                    pe.matmul(p_inp[1][:], wb_rep[:], chunk(xcT, c), start=True, stop=True).then_inc(s["b_ready"], 1)
                    wait(pe, "decayed", c, NG, 0)
                    pe.matmul(p_dec[1][:], wc_rep[:], chunk(xcT, c), start=True, stop=True).then_inc(s["c_ready"], 1)
                if ffn:
                    wait(pe, "yg_ready", f, 1, 1)
                    wait(pe, "res_ready", f, 1, 1)
                    pe.matmul(p_up[0][:], ones[:], bo_row[:].rearrange("p (j e) -> p j e", j=1).to_broadcast([1, JT, P]),
                              start=True, stop=True, skip_group_check=True)
                    for j in range(JT):
                        ins = pe.matmul(p_up[0][:, j * P:(j + 1) * P], yg[:, j * P:(j + 1) * P], wo_gT[:],
                                        start=False, stop=True, skip_group_check=True)
                    ins.then_inc(s["attn_ready"], 1)
                    wait(pe, "xn2", f, JT, JT)
                    for j in range(JT):
                        ins = pe.transpose(p_up[1][:, j * P:(j + 1) * P], xn[:, j, :], ident)
                    ins.then_inc(s["xn2_t"], 1)
                    wait(pe, "h2_ready", f, 1, 1)
                    wait(pe, "x2_ready", f, 1, 1)
                    for j in range(JT):
                        ins = pe.matmul(p_up[0][:, j * NE:(j + 1) * NE], h2[:, j * P:(j + 1) * P],
                                        small[:, C_ROUTE:C_ROUTE + NE], start=True, stop=True)
                    ins.then_inc(s["lg_ready"], 1)
                    wait(pe, "wr_ready", f, 3, 3)
                    for j in range(JT):
                        ins = pe.transpose(p_up[0][0:2 * NE, j * P:(j + 1) * P], wr[:, j, :], ident)
                    ins.then_inc(s["wrT_ready"], 1)
                    wait(pe, "wrT_copied", f, 1, 1)
                    for n in range(NE):
                        if n >= 2:
                            wait(pe, "wbc_copied", f, NE, n - 1)
                        pe.matmul(p_up[(n + 1) % 2][:], expert_pick[:, n, :], wrT[:], start=True,
                                  stop=True).then_inc(s["wbc_ready"], 1)
                for kind, k in ORDER:
                    if scan and kind == "decay":
                        g = GROUPS[k]
                        wait(pe, "d_lo", c, 2, 1 + g // 8)
                        if k == 1:
                            wait(pe, "cb_ready", c, 1, 1)
                        wait(pe, "decayed", c, NG, k - 1)
                        pe.matmul(p_dec[k % 2][:], pick[:, g % 8, :], delta_r[:, g // 8, :], start=True,
                                  stop=True).then_inc(s["dec_ready"], 1)
                    if scan and kind == "scan":
                        g = GROUPS[k]
                        wait(pe, "dx_lo", c, 2, 1 + g // 8)
                        if k == 0:
                            wait(pe, "zb", c, 1, 1)
                        if k == 1:
                            wait(pe, "bb_ready", c, 1, 1)
                        wait(pe, "scanned", c, NG, k - 1)
                        pe.matmul(p_inp[k % 2][:], pick[:, g % 8, :], dx_r[:, g // 8, :], start=True,
                                  stop=True).then_inc(s["inp_ready"], 1)
                    if scan and kind == "sum":
                        wait(pe, "hc_ready", c, NG, QB * (k + 1))
                        if k == 0:
                            wait(pe, "yg_ready", c, 1, 0)
                        for i in range(QB):
                            ins = pe.matmul(p_y[32 * i:32 * (i + 1), :],
                                            const[:, K_SUM + 32 * k:K_SUM + 32 * (k + 1)],
                                            hc[:, (QB * k + i) % (2 * QB), :], start=(k == 0), stop=(k == NG // QB - 1),
                                            tile_position=(0, 32 * i))
                        ins.then_inc(s["summed"], 1)
                    if ffn and kind == "up":
                        if k == 0:
                            wait(pe, "h2_lo_ready", f, 1, 1)
                            wait(pe, "wbc_copied", f, NE, NE)
                        if k > 0:
                            wait(pe, "silued", f, NH, k)
                        split_product(p_up[0], w0_hi, w0_lo, k, "gate_up")
                        if k > 0:
                            wait(pe, "multiplied", f, NH, k)
                        split_product(p_up[1], w1_hi, w1_lo, k, "lin_up")
                    if ffn and kind == "down":
                        wait(pe, "weighted", f, NH, k + 1)
                        pe.matmul(p_out[:], wo[:, k, :], mw[:, k % 4, :], start=(k == 0),
                                  stop=(k == NH - 1)).then_inc(s["down_done"], 1)
                if ffn:
                    wait(pe, "fo_ready", f, 1, 1)
                    wait(pe, "silued", f, NH, NH)
                    for j in range(JT):
                        ins = pe.matmul(p_up[0][:, j * P:(j + 1) * P], fo[:, j * P:(j + 1) * P], ident,
                                        is_transpose=True, start=True, stop=True)
                    ins.then_inc(s["foT_ready"], 1)

            pe.wait_ge(s["const_in"], 16)
            pe.wait_ge(s["wo_in"], 16)
            pe.wait_ge(s["w_lo"], 2)
            step(0, True, False)
            with pe.Fori(1, NC) as c:
                step(c, True, True)
            step(NC, False, True)


def kernel(L0_attn_x, L0_attn_conv_w, L0_attn_conv_b, L0_attn_Wd, L0_attn_bd, L0_attn_Wb, L0_attn_Wc,
           L0_attn_log_a, L0_attn_Wg, L0_attn_bg, L0_attn_Wo, L0_attn_bo, L0_ffn_gate_kernel,
           L0_ffn_w0_kernel, L0_ffn_w1_kernel, L0_ffn_wo_kernel, L0_c, L0_wmod):
    import numpy as np
    import concourse.bacc as bacc
    from concourse.bass_utils import run_bass_kernel_spmd

    def col(a):
        return np.asarray(a).reshape(D, -1)

    xa = np.asarray(L0_attn_x)
    n_tiles = xa.shape[1] // P
    loga = np.asarray(L0_attn_log_a).reshape(NG, GC, NS).transpose(2, 1, 0).reshape(P, NG)
    small = np.concatenate([col(L0_attn_conv_w), col(L0_attn_conv_b), col(L0_attn_bd), col(L0_attn_bg),
                            col(L0_attn_bo), col(L0_c), np.asarray(L0_ffn_gate_kernel), loga,
                            np.asarray(L0_attn_Wb).T, np.asarray(L0_attn_Wc).T], axis=1)
    dense = np.concatenate([np.asarray(L0_attn_Wd).T, np.asarray(L0_attn_Wg).T, np.asarray(L0_attn_Wo),
                            np.asarray(L0_wmod)], axis=1)
    const = np.zeros((P, N_CONST), np.float32)
    for p in range(P):
        const[p, K_ID + p] = 1.0
        const[p, K_FOLD + p % 64] = 1.0
        for q in range(4):
            const[p, K_SUM + 32 * q + GC * q + p % GC] = 1.0
        if p < 2 * NE:
            const[p, K_EXP + p % NE] = 1.0
        const[p, K_IOTA:K_IOTA + NE] = range(NE)
    arrays = {
        "x": xa.reshape(n_tiles, P, D).transpose(1, 0, 2).reshape(P, n_tiles * D),
        "small": small,
        "dense": dense,
        "const": const,
        "w0": np.asarray(L0_ffn_w0_kernel).transpose(1, 0, 2).reshape(D, NE * H),
        "w1": np.asarray(L0_ffn_w1_kernel).transpose(1, 0, 2).reshape(D, NE * H),
        "wo": np.asarray(L0_ffn_wo_kernel).reshape(NH, P, D).transpose(1, 0, 2).reshape(P, NH * D),
    }
    arrays = {k: np.ascontiguousarray(a) for k, a in arrays.items()}
    nc = bacc.Bacc("TRN2", target_bir_lowering=False, num_devices=1)
    args = [nc.dram_tensor(f"in_{k}", a.shape, F32, kind="ExternalInput").ap() for k, a in arrays.items()]
    args.append(nc.dram_tensor("out_tokens", (P, n_tiles * D), F32, kind="ExternalOutput").ap())
    program(nc, *args)
    r = run_bass_kernel_spmd(nc, [{f"in_{k}": a for k, a in arrays.items()}], core_ids=[0])
    got = r.results[0]["out_tokens"]
    return got.reshape(P, n_tiles, D).transpose(1, 0, 2).reshape(xa.shape)
```

```python
from contextlib import ExitStack

import concourse.bass as bass
from concourse import mybir

ALU = mybir.AluOpType
ACT = mybir.ActivationFunctionType
F32 = mybir.dt.float32
F32R = mybir.dt.float32r
U32 = mybir.dt.uint32

P = 128
TC = 512
NC = 4
JT = TC // P
D = 128
NS = 16
GC = P // NS
NG = D // GC
NE = 8
H = 256
NH = NE * H // P
HE = H // P
TAPS = 4
PAD = TAPS - 1
EPS = 1e-5
GATE_MIN = 0.25
ND = 8
NHC = 7
NU = 6
NQ = NE * H // TC
QB = 4

C_CONVW, C_CONVB, C_BD, C_BG, C_BO, C_C = 0, 4, 5, 6, 7, 8
C_ROUTE, C_LOGA, C_WB, C_WC = 9, 17, 33, 49
N_SMALL = 65
M_WD, M_WG, M_WO, M_MOD = 0, 128, 256, 384
N_DENSE = 384 + 6 * 128
K_ID, K_FOLD, K_SUM, K_IOTA = 0, 128, 192, 320
N_CONST = 328

GROUPS = [(k % QB) * (NG // QB) + k // QB for k in range(NG)]


ORDER = {
    "pe": """
        norm1:0 gate:0 z:0 c:0 proj norm1:1 b:0 decay:0 inp:0*2 decay:0 z:1 decay:0 inp:0 decay:0*2 inp:0*3
        decay:0 c:1 inp:0*2 decay:0 sum:0 decay:0 norm1:2 decay:0 inp:0*2 decay:0*2 inp:0 decay:0*2 inp:0
        decay:0*2 b:1 gate:1 decay:0 inp:0*2 sum:0 inp:0 decay:1 inp:0 decay:1*2 z:2 inp:1 decay:1 inp:1 sum:0
        inp:1 decay:1*2 sum:0 inp:1 decay:1 norm1:3 attn:0 inp:1 decay:1 inp:1 decay:1*4 sum:1 decay:1 inp:1*2
        norm2:0 decay:1 c:2 b:2 up:0 lin:0 inp:1 up:0 inp:1 gate:2 up:0 lin:0 up:0 inp:1 sum:1 inp:1 z:3 up:0
        lin:0 logits:0 inp:1 decay:1 lin:0 decay:1 up:0 decay:2 inp:1 lin:0 decay:2 b:3 down:0 lin:0 inp:1 up:0
        sum:1 inp:1 up:0 lin:0 decay:2 down:0 decay:2 up:0 decay:2*2 inp:2*2 lin:0 down:0 inp:2 decay:2*2 sum:1
        c:3 inp:2 lin:0 attn:1 up:0 lin:0 gate:3 up:0 inp:2*2 lin:0 up:0 down:0 lin:0 up:0 norm2:1 up:0 lin:0
        inp:2 up:0 inp:2 decay:2 lin:0 decay:2 down:0 inp:2 decay:2 up:0 lin:0 sum:2 logits:1 decay:2 lin:0 up:1
        inp:2 down:0 inp:2 decay:2 inp:2 sum:2 up:1 decay:2 lin:1 inp:2 down:0 decay:2 lin:1 up:1 sum:2 decay:2
        decay:3 up:1 lin:1 inp:2 up:1 inp:2 lin:1 down:0 inp:2 decay:3 up:1 lin:1 inp:3 decay:3*2 down:1
        decay:3*2 inp:3 lin:1 up:1 sum:2 up:1 lin:1 inp:3*2 up:1 down:1 lin:1 attn:2 up:1 decay:3*2 lin:1 up:1
        down:1 inp:3 lin:1 up:1 down:1 lin:1 decay:3 norm2:2 inp:3 lin:1 up:1 sum:3 lin:1 up:1 down:1 lin:1 up:1
        inp:3*2 lin:1 up:1 down:1 lin:1 up:2 logits:2 decay:3 up:2 lin:2 inp:3 up:2 inp:3 lin:2 up:2 down:1
        sum:3 inp:3 lin:2 decay:3 up:2 decay:3 lin:2 decay:3 down:1 lin:2 inp:3 up:2 decay:3 lin:2 up:2 down:2
        inp:3 up:2 lin:2 down:2 decay:3 inp:3 sum:3 up:2 lin:2 inp:3 up:2 decay:3 lin:2 down:2 inp:3 lin:2 up:2
        down:2 lin:2 up:2 sum:3 lin:2 up:2 attn:3 lin:2 up:2 down:2 lin:2 up:2 down:2 lin:2 norm2:3 up:2 lin:2
        down:2 up:3 lin:3 logits:3 up:3 lin:3 down:2 up:3 lin:3 down:3 up:3 lin:3 up:3 lin:3 up:3 lin:3 up:3
        lin:3 up:3 down:3 lin:3 up:3 lin:3 up:3 down:3 lin:3 up:3 down:3 lin:3 up:3 lin:3 up:3 down:3 up:3 lin:3
        up:3 lin:3 down:3 lin:3 up:3 down:3 lin:3 down:3""",
    "act": """
        tok1:0 norm1:0 picks weights:0 xc:0 gate:0 weights:0 z:0 soft:0 tok1:1 c:0 weights:0 norm1:1 split_d:0
        b:0 split_x:0 xc:1 decay:0*2 z:1 decay:0*2 soft:1 decay:0*2 c:1 tok1:2 decay:0*2 norm1:2 split_d:1
        decay:0*2 split_x:1 weights:0 decay:0*2 weights:0 decay:0*3 weights:0 b:1 gate:1 xc:2 decay:0 decay:1*2
        tok1:3 weights:0 decay:1 z:2 decay:1*2 weights:0 decay:1 soft:2 decay:1 norm1:3 decay:1*4 tok2:0
        decay:1*2 norm2:0 decay:1 up:0 c:2 b:2 up:0*2 split_d:2 xc:3 up:0 gate:2 split_x:2 z:3 up:0 decay:1*2
        decay:2*2 top:0 up:0*3 b:3 decay:2*3 soft:3 decay:2*3 up:0*4 c:3 gate:3 tok2:1 up:0*2 norm2:1 up:0
        decay:2*2 split_x:3 split_d:3 up:0 decay:2 top:1 decay:2 up:1*2 decay:2*3 up:1*3 decay:2 decay:3*4
        up:1*3 decay:3*2 up:1*3 decay:3*2 tok2:2 up:1*2 decay:3 up:1 norm2:2 up:1*2 up:2*3 decay:3 up:2 top:2
        decay:3*3 up:2*4 decay:3*2 up:2 decay:3 up:2*6 tok2:3 norm2:3 up:2 up:3*2 top:3 up:3*14""",
    "dve": """
        stat1:0 mods conv:0 stat1:1 fold proj stat1:2 delta:0 conv:1 split_d:0 split_x:0 stat1:3 mix:0*2
        scan:0*2 mix:0*2 scan:0*2 mix:0 carry:0 mix:0 scan:0*2 delta:1 mix:0*2 scan:0*2 mix:0 carry:0 mix:0
        split_d:1 scan:0*2 mix:0*2 scan:0*2 conv:2 carry:0 mix:0*2 scan:0*2 mix:0*2 scan:0 split_x:1 scan:0
        mix:1 carry:0 scan:1 mix:1*2 scan:1*2 gated:0 mix:1 scan:1 attn:0 carry:1 stat2:0 mix:1*2 scan:1*2
        mix:1*2 delta:2 scan:1*2 conv:3 lin:0 carry:1 mix:1*2 scan:1*2 lin:0 mix:1*2 scan:1*2 lin:0 split_d:2
        logits:0 lin:0 carry:1 mix:1*2 scan:1*2 lin:0 route:0 lin:0 down:0 mix:1*2 scan:1 lin:0 scan:1 split_x:2
        carry:1 down:0 mix:2*2 scan:2 lin:0 mix:2 scan:2*2 gated:1 down:0 lin:0 mix:2 attn:1 scan:2 lin:0
        stat2:1 mix:2 carry:2 lin:0 delta:3 mix:2 lin:0 scan:2*2 lin:0 down:0 mix:2 scan:2 mix:2 lin:0 scan:2
        mix:2 down:0 carry:2 lin:0 scan:2 split_x:3 logits:1 mix:2 scan:2 lin:0 mix:2*2 down:0 scan:2*2 mix:2
        lin:1 carry:2 split_d:3 lin:1 route:1 scan:2 lin:1 down:0 mix:2 scan:2 mix:2 lin:1 scan:2 down:0 mix:2
        mix:3 scan:2 lin:1 carry:2 scan:3 lin:1 mix:3 down:1 scan:3 gated:2 lin:1 mix:3*2 scan:3 down:1 lin:1
        scan:3 lin:1 attn:2 stat2:2 down:1 lin:1 carry:3 mix:3 scan:3 down:1 lin:1 mix:3 lin:1*2 scan:3 lin:1
        down:1 mix:3*2 lin:1 scan:3*2 carry:3 lin:1 down:1 logits:2 lin:2 mix:3*2 scan:3*2 lin:2 mix:3 lin:2
        down:1 lin:2 route:2 lin:2 down:1 lin:2 mix:3 scan:3 down:2 scan:3 carry:3 mix:3 lin:2 scan:3 mix:3
        down:2 lin:2 mix:3 scan:3 lin:2 scan:3 down:2 mix:3 scan:3 lin:2*2 down:2 gated:3 lin:2 attn:3 lin:2
        stat2:3 down:2 lin:2*2 down:2 lin:2 lin:3 down:2 lin:3 logits:3 down:2 route:3 lin:3*3 down:3 lin:3
        carry:3 lin:3*2 down:3 lin:3 down:3 lin:3*2 down:3 lin:3*2 down:3 lin:3 down:3 lin:3 down:3 lin:3 down:3""",
    "pool": """
        stat1:0 stat1:1 weights:0 soft:0 delta:0 bias:0 stat1:2 wo:0 scan:0*2 weights:0 soft:1 scan:0*2
        weights:0 scan:0*2 delta:1 scan:0*3 weights:0*2 stat1:3 weights:0 scan:0*7 scan:1*2 soft:2 scan:1*2
        stat2:0 weights:0*2 scan:1 norm2:0 scan:1 delta:2 scan:1*2 wo:0*2 bias:1 scan:1 wo:0 bias:2 scan:1*4
        down:0 scan:1*3 down:0*2 soft:3 stat2:1 scan:2*4 delta:3 norm2:1 scan:2*5 down:0 scan:2 down:0*2
        scan:2*4 down:0 scan:2 down:0 scan:2 scan:3*3 down:1 scan:3 down:1 stat2:2 down:1*2 scan:3*2 norm2:2
        scan:3*3 down:1*3 scan:3 down:1 scan:3 down:2 scan:3*2 bias:3 scan:3*3 down:2*2 stat2:3 down:2 norm2:3
        down:2*4 down:3*8""",
}

ACT_KINDS = ("norm1", "gate", "z", "b", "c", "decay", "norm2")
DVE_KINDS = ("inp", "attn", "logits")


def pieces(engine):
    found = []
    for word in ORDER[engine].split():
        name, _, count = word.partition("*")
        kind, _, c = name.partition(":")
        for _ in range(int(count or 1)):
            k = sum(p[:2] == (kind, int(c or 0)) for p in found)
            found.append((kind, int(c or 0), k))
    return found


def program(nc, x_in, small_in, dense_in, const_in, w0_in, w1_in, wo_in, out):
    assert x_in.shape[1] == NC * TC

    def turns(kinds):
        return {p: n for n, p in enumerate([p for p in pieces("pe") if p[0] in kinds])}

    act_turn = turns(ACT_KINDS)
    dve_turn = turns(DVE_KINDS)

    with ExitStack() as ctx:
        def sb(name, shape, dt=F32):
            return ctx.enter_context(nc.sbuf_tensor(name, shape, dt))

        x = sb("x", [P, NC * TC])
        small = sb("small", [P, N_SMALL])
        dense = sb("dense", [P, N_DENSE])
        const = sb("const", [P, N_CONST])
        hT = sb("hT", [P, PAD + NC * TC])
        xc = sb("xc", [P, TC])
        gth = sb("gth", [P, 2, TC])
        decay = sb("decay", [P, ND, TC])
        w0_hi = sb("w0_hi", [P, NE * H], F32R)
        w0_lo = sb("w0_lo", [P, NE * H], F32R)
        w1_hi = sb("w1_hi", [P, NE * H], F32R)
        w1_lo = sb("w1_lo", [P, NE * H], F32R)
        wo = sb("wo", [P, NH, D])
        pick = sb("pick", [P, 8, P], F32R)
        wb_rep = sb("wb_rep", [P, P])
        wc_rep = sb("wc_rep", [P, P])
        wo_g = sb("wo_g", [P, P])
        wo_gT = sb("wo_gT", [P, P])
        rows = sb("rows", [P, 2, P])
        cvec = sb("cvec", [P, 32])
        neg_a = sb("neg_a", [P, NG])
        state = sb("state", [P, NG])
        stats = sb("stats", [P, JT, 6])
        mv1 = sb("mv1", [P, JT, 2])
        mv2 = sb("mv2", [P, JT, 2])
        veps1 = sb("veps1", [P, JT])
        veps2 = sb("veps2", [P, JT])
        mneg1 = sb("mneg1", [P, JT])
        mneg2 = sb("mneg2", [P, JT])
        shift1 = sb("shift1", [P, JT])
        shift2 = sb("shift2", [P, JT])
        rstd1 = sb("rstd1", [P, JT])
        rstd2 = sb("rstd2", [P, JT])
        mhalf = sb("mhalf", [P, JT])
        xn1 = sb("xn1", [P, JT, P])
        xn2 = sb("xn2", [P, JT, P])
        zbuf = sb("zbuf", [P, 2, TC])
        za, zr = zbuf[:, 0, :], zbuf[:, 1, :]
        acc = zbuf
        ze = sb("ze", [P, TC])
        zu = sb("zu", [P, TC])
        zl = sb("zl", [P, TC])
        delta = sb("delta", [P, TC])
        dx = sb("dx", [P, TC])
        delta_r = sb("delta_r", [P, 2, 2, TC], F32R)
        dx_r = sb("dx_r", [P, 2, 2, TC], F32R)
        bb = sb("bb", [P, 2, TC])
        cb = sb("cb", [P, 2, TC])
        h = sb("h", [P, QB, TC])
        hc = sb("hc", [P, NHC, TC])
        yg = sb("yg", [P, TC])
        h2 = sb("h2", [P, TC])
        h2_hi = sb("h2_hi", [P, 2, TC], F32R)
        h2_lo = sb("h2_lo", [P, 2, TC], F32R)
        lg = sb("lg", [P, JT, NE])
        top = sb("top", [P, JT, 8])
        topi = sb("topi", [P, JT, 8], U32)
        gt = sb("gt", [P, 6, JT, NE])
        weights = sb("weights", [P, 2, JT, NE])
        w_raw = sb("w_raw", [P, 2 * NE * H])
        silu_up = sb("silu_up", [P, 2, TC])
        part = sb("part", [P, 2, JT, P])
        hid = sb("hid", [P, NU, TC])

        def bank(name):
            return ctx.enter_context(nc.psum_tensor(name, [P, TC], F32))

        p_act = [bank("p_act0"), bank("p_act1")]
        p_dve = [bank("p_dve0"), bank("p_dve1")]
        p_y = bank("p_y")
        p_gate = bank("p_gate")
        p_lin = bank("p_lin")
        p_out = bank("p_out")

        ident = const[:, K_ID:K_ID + P]
        wdT = dense[:, M_WD:M_WD + P]
        wgT = dense[:, M_WG:M_WG + P]
        wo_attn = dense[:, M_WO:M_WO + P]
        sa, one_ca, sb_, one_cb = (cvec[:, i:i + 1] for i in range(4))
        ga, gb = cvec[:, 4:5], cvec[:, 5:6]
        half_bg = cvec[:, 20:21]
        silu_c = cvec[:, 21:22]
        bo_g = cvec[:, 22:23]

        names = """const_in small_in x0_in x_in mod_in dense_in w0_in w1_in wo_in
            dve_set act_set pe_set pool_set picked w_hi w_lo wo_ready mod_ready fold_ready proj_ready proj_taken
            act_full act_free dve_full
            stat1 aggr1 eps1 shift1 rstd1_ready xn1_ready biased tap conv_done xc_ready
            za_ready ze_ready zu_ready zl_ready soft_step delta_ready dx_ready
            d_hi d_lo dx_hi dx_lo
            mixed scanned carried hc_ready summed yg_ready
            x2_ready stat2 aggr2 eps2 shift2 rstd2_ready xn2_ready h2_hi_ready h2_lo_ready
            lg_copied top_ready topi_ready route_diff route_exp route_step wt_ready
            gate_up lin_up silued multiplied down_done part_ready added out_done""".split()
        s = {n: ctx.enter_context(nc.semaphore("s_" + n)) for n in names}

        def chunk(t, c, off=0, n=TC):
            return t[:, c * TC + off:c * TC + off + n]

        block = ctx.enter_context(nc.Block())

        @block.sync
        def _(sp):
            sp.dma_start(chunk(x, 0), chunk(x_in, 0)).then_inc(s["x0_in"], 16)
            sp.dma_start(small[:], small_in).then_inc(s["small_in"], 16)
            sp.dma_start(dense[:, M_MOD:N_DENSE], dense_in[:, M_MOD:N_DENSE]).then_inc(s["mod_in"], 16)
            sp.dma_start(const[:], const_in).then_inc(s["const_in"], 16)
            sp.dma_start(dense[:, 0:M_MOD], dense_in[:, 0:M_MOD]).then_inc(s["dense_in"], 16)
            sp.dma_start(w_raw[:, 0:NE * H], w0_in).then_inc(s["w0_in"], 16)
            sp.dma_start(x[:, TC:NC * TC], x_in[:, TC:NC * TC]).then_inc(s["x_in"], 16)
            sp.dma_start(w_raw[:, NE * H:2 * NE * H], w1_in).then_inc(s["w1_in"], 16)
            sp.dma_start(wo[:].rearrange("p a e -> p (a e)"), wo_in).then_inc(s["wo_in"], 16)
            for c in range(NC):
                sp.wait_ge(s["added"], NE * (c + 1))
                sp.dma_start(chunk(out, c), chunk(x, c)).then_inc(s["out_done"], 16)
            sp.wait_ge(s["out_done"], 16 * NC)

        @block.scalar
        def _(act):
            loaded = [None]

            def table(name):
                if loaded[0] != name:
                    act.preload_act_table_set(name)
                    loaded[0] = name

            def silu_table():
                table("silu_and_others")

            def exp_table():
                table("natural_log_exp_and_others")

            silu_table()
            act.wait_ge(s["small_in"], 16)
            nc.scalar.activation(silu_c, small[:, C_C:C_C + 1], ACT.Silu).then_inc(s["act_set"], 1)

            def full(piece):
                act.wait_ge(s["act_full"], act_turn[piece] + 1)
                return p_act[act_turn[piece] % 2]

            for kind, c, k in pieces("act"):
                n = c * NG + k
                piece = (kind, c, k)
                if kind in ("tok1", "tok2"):
                    q = kind[3]
                    xn, rstd, shift = (xn1, rstd1, shift1) if q == "1" else (xn2, rstd2, shift2)
                    act.wait_ge(s["shift" + q], c + 1)
                    if c > 0:
                        act.wait_ge(s["act_full"], act_turn["norm" + q, c - 1, 0] + 1)
                    for j in range(JT):
                        nc.scalar.activation(xn[:, j, :], chunk(x, c, j * P, P), ACT.Identity, bias=shift[:, j:j + 1],
                                             scale=rstd[:, j:j + 1]).then_inc(s[f"xn{q}_ready"], 1)
                if kind == "norm1":
                    bank_ = full(piece)
                    act.wait_ge(s["mod_ready"], 1)
                    nc.scalar.activation(chunk(hT, c, PAD), bank_[:], ACT.Identity, bias=sa,
                                         scale=one_ca).then_inc(s["act_free"], 1)
                if kind == "gate":
                    silu_table()
                    bank_ = full(piece)
                    act.wait_ge(s["dve_set"], 3)
                    if c - 1 > 0:
                        act.wait_ge(s["yg_ready"], c - 1)
                    nc.scalar.activation(gth[:, c % 2, :], bank_[:], ACT.Tanh, bias=half_bg,
                                         scale=0.5).then_inc(s["act_free"], 1)
                if kind == "xc":
                    silu_table()
                    act.wait_ge(s["conv_done"], c + 1)
                    if c > 0:
                        act.wait_ge(s["dx_ready"], c)
                    if c > 0:
                        act.wait_ge(s["act_full"], max(act_turn[kind, c - 1, 0] for kind in ("z", "b", "c")) + 1)
                    nc.scalar.activation(xc[:], acc[:, 1, :], ACT.Silu,
                                         bias=small[:, C_CONVB:C_CONVB + 1]).then_inc(s["xc_ready"], 1)
                if kind == "z":
                    bank_ = full(piece)
                    bd = small[:, C_BD:C_BD + 1]
                    nc.scalar.activation(za, bank_[:], ACT.Abs, bias=bd).then_inc(s["za_ready"], 1)
                    nc.scalar.activation(zr, bank_[:], ACT.Relu, bias=bd).then_inc(s["act_free"], 1)
                if kind == "b":
                    bank_ = full(piece)
                    if (c - 1) * NG > 0:
                        act.wait_ge(s["mixed"], (c - 1) * NG)
                    nc.scalar.copy(bb[:, c % 2, :], bank_[:]).then_inc(s["act_free"], 1)
                if kind == "c":
                    bank_ = full(piece)
                    if (c - 1) * NG > 0:
                        act.wait_ge(s["hc_ready"], (c - 1) * NG)
                    nc.scalar.copy(cb[:, c % 2, :], bank_[:]).then_inc(s["act_free"], 1)
                if kind == "soft":
                    exp_table()
                    act.wait_ge(s["za_ready"], c + 1)
                    nc.scalar.activation(ze[:], za, ACT.Exp, scale=-1.0).then_inc(s["ze_ready"], 1)
                    if c == 0:
                        nc.scalar.activation(neg_a[:], small[:, C_LOGA:C_LOGA + NG], ACT.Exp).then_inc(s["act_set"], 1)
                    act.wait_ge(s["ze_ready"], c + 1)
                    nc.scalar.activation(zl[:], ze[:], ACT.Ln, bias=1.0).then_inc(s["zl_ready"], 1)
                for split, src, dst, ready, used, hi in (
                        ("split_d", delta, delta_r, "delta_ready", "scanned", "d_hi"),
                        ("split_x", dx, dx_r, "dx_ready", "mixed", "dx_hi")):
                    if kind == split:
                        act.wait_ge(s[ready], c + 1)
                        if (c - 1) * NG > 0:
                            act.wait_ge(s[used], (c - 1) * NG)
                        nc.scalar.copy(dst[0:64, c % 2, 0, :], src[0:64, :]).then_inc(s[hi], 1)
                        nc.scalar.copy(dst[64:128, c % 2, 1, :], src[64:128, :]).then_inc(s[hi], 1)
                        if kind == "split_d" and c == 0:
                            act.wait_ge(s["act_set"], 2)
                            nc.scalar.mul(neg_a[:], neg_a[:], -1.0).then_inc(s["act_set"], 1)
                if kind == "decay":
                    exp_table()
                    bank_ = full(piece)
                    act.wait_ge(s["act_set"], 3)
                    if n - ND + 1 > 0:
                        act.wait_ge(s["scanned"], n - ND + 1)
                    g = GROUPS[k]
                    nc.scalar.activation(decay[:, n % ND, :], bank_[:], ACT.Exp,
                                         scale=neg_a[:, g:g + 1]).then_inc(s["act_free"], 1)
                if kind == "norm2":
                    bank_ = full(piece)
                    if c > 0:
                        act.wait_ge(s["h2_lo_ready"], c)
                    if c > 0:
                        act.wait_ge(s["lg_copied"], c)
                    nc.scalar.activation(h2[:], bank_[:], ACT.Identity, bias=sb_,
                                         scale=one_cb).then_inc(s["act_free"], 1)
                    act.wait_ge(s["act_free"], act_turn[piece] + 1)
                    if (c - 1) * NH > 0:
                        act.wait_ge(s["multiplied"], (c - 1) * NH)
                    nc.scalar.copy(h2_hi[:, c % 2, :], h2[:]).then_inc(s["h2_hi_ready"], 1)
                if kind == "top":
                    exp_table()
                    act.wait_ge(s["route_diff"], c + 1)
                    nc.scalar.activation(gt[:, 0, :, 1:2], gt[:, 0, :, 0:1], ACT.Exp,
                                         scale=-1.0).then_inc(s["route_exp"], 1)
                if kind == "up":
                    silu_table()
                    act.wait_ge(s["gate_up"], n + 1)
                    if n - 1 > 0:
                        act.wait_ge(s["multiplied"], n - 1)
                    nc.scalar.activation(silu_up[:, k % 2, :], p_gate[:], ACT.Silu).then_inc(s["silued"], 1)
                if kind == "picks":
                    act.wait_ge(s["const_in"], 16)
                    for g in range(8):
                        src = const[:, K_FOLD + g * GC:K_FOLD + (g + 1) * GC].rearrange(
                            "p (n i) -> p n i", n=1).to_broadcast([P, NS, GC])
                        nc.scalar.copy(pick[:, g, :].rearrange("p (n i) -> p n i", i=GC), src).then_inc(
                            s["picked"], 1)
                if kind == "weights":
                    hi, cols = (w0_hi, w1_hi)[k // NQ], slice(k % NQ * TC, (k % NQ + 1) * TC)
                    act.wait_ge(s["w0_in" if k < NQ else "w1_in"], 16)
                    nc.scalar.copy(hi[:, cols], w_raw[:, k * TC:(k + 1) * TC]).then_inc(s["w_hi"], 1)

        @block.vector
        def _(dve):
            n_set = 0

            def setup(ins):
                nonlocal n_set
                n_set += 1
                ins.then_inc(s["dve_set"], 1)

            def settle():
                dve.wait_ge(s["dve_set"], n_set)

            def full(piece):
                dve.wait_ge(s["dve_full"], dve_turn[piece] + 1)
                return p_dve[dve_turn[piece] % 2]

            def statistics(name, c, mv, veps, mneg):
                for j in range(JT):
                    dve.bn_stats(stats[:, j, :], chunk(x, c, j * P, P)).then_inc(s["stat" + name], 1)
                dve.wait_ge(s["stat" + name], JT * (c + 1))
                for j in range(JT):
                    dve.bn_aggr(mv[:, j, :], stats[:, j, :]).then_inc(s["aggr" + name], 1)
                dve.wait_ge(s["aggr" + name], JT * (c + 1))
                if c > 0:
                    dve.wait_ge(s["shift" + name], c)
                dve.tensor_scalar(veps[:], mv[:, :, 1], EPS, None, ALU.add).then_inc(s["eps" + name], 1)
                dve.tensor_scalar(mneg[:], mv[:, :, 0], -1.0, None, ALU.mult).then_inc(s["eps" + name], 1)

            setup(dve.memset(state[:], 0.0))
            setup(dve.memset(hT[:, 0:PAD], 0.0))
            dve.wait_ge(s["small_in"], 16)
            setup(dve.tensor_scalar(half_bg, small[:, C_BG:C_BG + 1], 0.5, None, ALU.mult))
            for rep, col in ((wb_rep, C_WB), (wc_rep, C_WC)):
                src = small[:, col:col + NS].rearrange("p (n i) -> p n i", i=1).to_broadcast([P, NS, GC])
                setup(dve.tensor_copy(rep[:].rearrange("p (n i) -> p n i", i=GC), src))
            for kind, c, k in pieces("dve"):
                n = c * NG + k
                piece = (kind, c, k)
                if kind == "stat1":
                    dve.wait_ge(s["x_in" if c else "x0_in"], 16)
                    statistics("1", c, mv1, veps1, mneg1)
                if kind == "mods":
                    dve.wait_ge(s["pe_set"], 1)
                    setup(dve.tensor_copy(cvec[:, 0:6], p_out[:, 0:6]))
                    settle()
                    setup(dve.tensor_scalar(cvec[:, 1:4:2], cvec[:, 1:4:2], 1.0, None, ALU.add))
                    setup(dve.tensor_scalar(cvec[:, 8:10], cvec[:, 4:6], 0.0, 2.0, ALU.is_ge, ALU.mult))
                    setup(dve.scalar_tensor_tensor(cvec[:, 10:12], cvec[:, 4:6], -1.0, cvec[:, 4:6], ALU.mult, ALU.max))
                    settle()
                    setup(dve.tensor_scalar(cvec[:, 12:14], cvec[:, 10:12], GATE_MIN, None, ALU.max))
                    settle()
                    dve.scalar_tensor_tensor(cvec[:, 4:6], cvec[:, 8:10], -1.0, cvec[:, 12:14], ALU.add,
                                             ALU.mult).then_inc(s["mod_ready"], 1)
                if kind == "fold":
                    dve.wait_ge(s["dense_in"], 16)
                    dve.wait_ge(s["mod_ready"], 1)
                    dve.tensor_scalar(wo_g[:], wo_attn, ga, 0.5, ALU.mult, ALU.mult).then_inc(s["fold_ready"], 1)
                    dve.tensor_scalar(bo_g, small[:, C_BO:C_BO + 1], ga, None, ALU.mult).then_inc(s["fold_ready"], 1)
                if kind == "proj":
                    dve.wait_ge(s["proj_ready"], 1)
                    dve.tensor_copy(wo_gT[:], p_y[:, 0:P]).then_inc(s["proj_taken"], 1)
                    dve.tensor_copy(rows[:], p_y[:, P:3 * P].rearrange("p (r e) -> p r e", r=2)
                                    ).then_inc(s["proj_taken"], 1)
                if kind == "conv":
                    dve.wait_ge(s["act_free"], act_turn["norm1", c, 0] + 1)
                    if c > 0:
                        dve.wait_ge(s["zl_ready"], c)
                    if c > 0:
                        dve.wait_ge(s["delta_ready"], c)
                    for t in range(TAPS):
                        w = small[:, C_CONVW + t:C_CONVW + t + 1]
                        if t == 0:
                            ins = dve.tensor_scalar(acc[:, 0, :], chunk(hT, c), w, None, ALU.mult)
                        else:
                            if (TAPS - 1) * c + t > 0:
                                dve.wait_ge(s["tap"], (TAPS - 1) * c + t)
                            ins = dve.scalar_tensor_tensor(acc[:, t % 2, :], chunk(hT, c, t), w, acc[:, 1 - t % 2, :],
                                                           ALU.mult, ALU.add)
                        ins.then_inc(s["tap" if t < TAPS - 1 else "conv_done"], 1)
                if kind == "delta":
                    dve.wait_ge(s["zu_ready"], c + 1)
                    if 2 * c > 0:
                        dve.wait_ge(s["d_hi"], 2 * c)
                    dve.scalar_tensor_tensor(za, zu[:], -1.0, ze[:], ALU.add, ALU.subtract).then_inc(s["soft_step"], 1)
                    dve.wait_ge(s["soft_step"], 2 * c + 1)
                    dve.wait_ge(s["zl_ready"], c + 1)
                    dve.tensor_tensor(zl[:], zl[:], za, ALU.subtract).then_inc(s["soft_step"], 1)
                    dve.wait_ge(s["soft_step"], 2 * c + 2)
                    dve.tensor_tensor(delta[:], zl[:], zr, ALU.add).then_inc(s["delta_ready"], 1)
                for split, src, dst, hi, lo in (("split_d", delta, delta_r, "d_hi", "d_lo"),
                                                ("split_x", dx, dx_r, "dx_hi", "dx_lo")):
                    if kind == split:
                        dve.wait_ge(s[hi], 2 * c + 1)
                        dve.tensor_tensor(dst[64:128, c % 2, 0, :], src[0:64, :], dst[0:64, c % 2, 0, :].bitcast(F32),
                                          ALU.subtract).then_inc(s[lo], 1)
                        dve.wait_ge(s[hi], 2 * c + 2)
                        dve.tensor_tensor(dst[0:64, c % 2, 1, :], src[64:128, :],
                                          dst[64:128, c % 2, 1, :].bitcast(F32), ALU.subtract).then_inc(s[lo], 1)
                if kind == "mix":
                    bank_ = full(("inp", c, k))
                    dve.wait_ge(s["act_free"], act_turn["b", c, 0] + 1)
                    dve.tensor_tensor(bank_[:], bank_[:], bb[:, c % 2, :], ALU.mult).then_inc(s["mixed"], 1)
                if kind == "scan":
                    bank_ = p_dve[dve_turn["inp", c, k] % 2]
                    dve.wait_ge(s["mixed"], n + 1)
                    dve.wait_ge(s["act_free"], act_turn["decay", c, k] + 1)
                    if n // QB > 0:
                        dve.wait_ge(s["carried"], n // QB)
                    if n - QB + 1 > 0:
                        dve.wait_ge(s["hc_ready"], n - QB + 1)
                    dve.tensor_tensor_scan(h[:, k % QB, :], decay[:, n % ND, :], bank_[:], state[:, k:k + 1],
                                           ALU.mult, ALU.add).then_inc(s["scanned"], 1)
                if kind == "carry":
                    dve.wait_ge(s["scanned"], c * NG + QB * (k + 1))
                    dve.tensor_copy(state[:, QB * k:QB * (k + 1)], h[:, :, TC - 1]).then_inc(s["carried"], 1)
                if kind == "gated":
                    dve.wait_ge(s["summed"], (c + 1) * NG // QB)
                    if c > 0:
                        dve.wait_ge(s["dve_full"], dve_turn["attn", c - 1, 0] + 1)
                    dve.scalar_tensor_tensor(yg[:], gth[:, c % 2, :], 1.0, p_y[:], ALU.add,
                                             ALU.mult).then_inc(s["yg_ready"], 1)
                if kind == "attn":
                    dve.wait_ge(s["biased"], c + 1)
                    dve.tensor_tensor(chunk(x, c), chunk(x, c), full(piece)[:], ALU.add).then_inc(s["x2_ready"], 1)
                if kind == "stat2":
                    dve.wait_ge(s["x2_ready"], c + 1)
                    statistics("2", c, mv2, veps2, mneg2)
                if kind == "logits":
                    dve.tensor_copy(lg[:], full(piece)[:, 0:JT * NE].rearrange("p (j n) -> p j n", n=NE)
                                    ).then_inc(s["lg_copied"], 1)
                    dve.wait_ge(s["lg_copied"], c + 1)
                    for j in range(JT):
                        dve.max(top[:, j, :], lg[:, j, :]).then_inc(s["top_ready"], 1)
                    dve.wait_ge(s["top_ready"], JT * (c + 1))
                    dve.tensor_tensor(gt[:, 0, :, 0:1], top[:, :, 0:1], top[:, :, 1:2],
                                      ALU.subtract).then_inc(s["route_diff"], 1)
                    for j in range(JT):
                        dve.max_index(topi[:, j, :], top[:, j, :], lg[:, j, :]).then_inc(s["topi_ready"], 1)
                if kind == "route":
                    dve.wait_ge(s["const_in"], 16)
                    dve.wait_ge(s["topi_ready"], JT * (c + 1))
                    dve.wait_ge(s["route_exp"], c + 1)
                    links = 8

                    def step(number, ins):
                        ins.then_inc(s["route_step"], 1)

                    def after(number):
                        if links * c + number > 0:
                            dve.wait_ge(s["route_step"], links * c + number)

                    iota = const[:, K_IOTA:K_IOTA + NE].rearrange("p (j n) -> p j n", j=1).to_broadcast([P, JT, NE])
                    step(1, dve.tensor_scalar(gt[:, 0, :, 2:3], gt[:, 0, :, 1:2], 1.0, None, ALU.add))
                    step(2, dve.tensor_copy(gt[:, 1, :, 0:2], topi[:, :, 0:2]))
                    after(1)
                    step(3, dve.reciprocal(gt[:, 0, :, 3:4], gt[:, 0, :, 2:3]))
                    after(2)
                    for i in range(2):
                        step(4 + i, dve.tensor_tensor(
                            gt[:, 2 + i], iota, gt[:, 1, :, i:i + 1].to_broadcast([P, JT, NE]), ALU.is_equal))
                    after(3)
                    step(6, dve.tensor_tensor(gt[:, 0, :, 4:5], gt[:, 0, :, 1:2], gt[:, 0, :, 3:4], ALU.mult))
                    after(5)
                    step(7, dve.tensor_tensor(gt[:, 4], gt[:, 2], gt[:, 0, :, 3:4].to_broadcast([P, JT, NE]),
                                              ALU.mult))
                    after(6)
                    step(8, dve.tensor_tensor(gt[:, 5], gt[:, 3], gt[:, 0, :, 4:5].to_broadcast([P, JT, NE]),
                                              ALU.mult))
                    after(8)
                    dve.tensor_tensor(weights[:, c % 2], gt[:, 4], gt[:, 5], ALU.add).then_inc(s["wt_ready"], 1)
                if kind == "lin":
                    dve.wait_ge(s["lin_up"], n + 1)
                    dve.wait_ge(s["silued"], n + 1)
                    if (n - NU) // HE + 1 > 0:
                        dve.wait_ge(s["down_done"], (n - NU) // HE + 1)
                    dve.tensor_tensor(hid[:, n % NU, :], silu_up[:, k % 2, :], p_lin[:],
                                      ALU.mult).then_inc(s["multiplied"], 1)
                if kind == "down":
                    expert = c * NE + k
                    dve.wait_ge(s["down_done"], expert + 1)
                    dve.wait_ge(s["wt_ready"], c + 1)
                    if expert - 1 > 0:
                        dve.wait_ge(s["added"], expert - 1)
                    dve.tensor_tensor(part[:, expert % 2], p_out[:].rearrange("p (j e) -> p j e", j=JT),
                                      weights[:, c % 2, :, k:k + 1].to_broadcast([P, JT, P]),
                                      ALU.mult).then_inc(s["part_ready"], 1)

        @block.gpsimd
        def _(pool):
            pool.memset(mhalf[:], -0.5).then_inc(s["pool_set"], 1)
            for kind, c, k in pieces("pool"):
                n = c * NG + k
                if kind == "stat1":
                    pool.wait_ge(s["eps1"], 2 * (c + 1))
                    if JT * c > 0:
                        pool.wait_ge(s["xn1_ready"], JT * c)
                    pool.wait_ge(s["pool_set"], 1)
                    pool.tensor_tensor(rstd1[:], veps1[:], mhalf[:], ALU.pow).then_inc(s["rstd1_ready"], 1)
                    pool.wait_ge(s["rstd1_ready"], c + 1)
                    pool.tensor_tensor(shift1[:], mneg1[:], rstd1[:], ALU.mult).then_inc(s["shift1"], 1)
                if kind == "stat2":
                    pool.wait_ge(s["eps2"], 2 * (c + 1))
                    if JT * c > 0:
                        pool.wait_ge(s["xn2_ready"], JT * c)
                    pool.wait_ge(s["pool_set"], 1)
                    pool.tensor_tensor(rstd2[:], veps2[:], mhalf[:], ALU.pow).then_inc(s["rstd2_ready"], 1)
                    pool.wait_ge(s["rstd2_ready"], c + 1)
                    pool.tensor_tensor(shift2[:], mneg2[:], rstd2[:], ALU.mult).then_inc(s["shift2"], 1)
                if kind == "soft":
                    pool.wait_ge(s["ze_ready"], c + 1)
                    pool.tensor_scalar(zu[:], ze[:], 1.0, 1.0, ALU.add, ALU.mult).then_inc(s["zu_ready"], 1)
                if kind == "delta":
                    pool.wait_ge(s["delta_ready"], c + 1)
                    pool.wait_ge(s["xc_ready"], c + 1)
                    if 2 * c > 0:
                        pool.wait_ge(s["dx_lo"], 2 * c)
                    pool.tensor_tensor(dx[:], delta[:], xc[:], ALU.mult).then_inc(s["dx_ready"], 1)
                if kind == "scan":
                    pool.wait_ge(s["scanned"], n + 1)
                    pool.wait_ge(s["act_free"], act_turn["c", c, 0] + 1)
                    if (n - NHC) // QB + 1 > 0:
                        pool.wait_ge(s["summed"], (n - NHC) // QB + 1)
                    pool.tensor_tensor(hc[:, n % NHC, :], h[:, k % QB, :], cb[:, c % 2, :],
                                       ALU.mult).then_inc(s["hc_ready"], 1)
                if kind == "bias":
                    pool.wait_ge(s["xn1_ready"], JT * (c + 1))
                    pool.wait_ge(s["proj_taken"], 2)
                    pool.tensor_tensor(chunk(x, c).rearrange("p (j e) -> p j e", j=JT),
                                       chunk(x, c).rearrange("p (j e) -> p j e", j=JT),
                                       rows[:, 0:1, :].to_broadcast([P, JT, P]), ALU.add).then_inc(s["biased"], 1)
                if kind == "norm2":
                    pool.wait_ge(s["h2_hi_ready"], c + 1)
                    pool.tensor_tensor(h2_lo[:, c % 2, :], h2[:], h2_hi[:, c % 2, :].bitcast(F32),
                                       ALU.subtract).then_inc(s["h2_lo_ready"], 1)
                if kind == "weights":
                    hi, lo = ((w0_hi, w0_lo), (w1_hi, w1_lo))[k // NQ]
                    cols = slice(k % NQ * TC, (k % NQ + 1) * TC)
                    pool.wait_ge(s["w_hi"], k + 1)
                    pool.tensor_tensor(lo[:, cols], w_raw[:, k * TC:(k + 1) * TC], hi[:, cols].bitcast(F32),
                                       ALU.subtract).then_inc(s["w_lo"], 1)
                if kind == "down":
                    expert = c * NE + k
                    tiles = chunk(x, c).rearrange("p (j e) -> p j e", j=JT)
                    pool.wait_ge(s["part_ready"], expert + 1)
                    if expert > 0:
                        pool.wait_ge(s["added"], expert)
                    pool.tensor_tensor(tiles, tiles, part[:, expert % 2], ALU.add).then_inc(s["added"], 1)
                if kind == "wo":
                    tiles = wo[:, k * NH // NQ:(k + 1) * NH // NQ, :]
                    pool.wait_ge(s["wo_in"], 16)
                    pool.wait_ge(s["proj_taken"], 2)
                    pool.tensor_tensor(tiles, tiles, rows[:, 1:2, :].to_broadcast([P, NH // NQ, P]),
                                       ALU.mult).then_inc(s["wo_ready"], 1)

        @block.tensor
        def _(pe):
            dve_pieces = list(dve_turn)

            def act_bank(piece):
                turn = act_turn[piece]
                if turn - 1 > 0:
                    pe.wait_ge(s["act_free"], turn - 1)
                return p_act[turn % 2]

            def dve_bank(piece):
                turn = dve_turn[piece]
                if turn >= 2:
                    held, c, k = dve_pieces[turn - 2]
                    if held == "inp":
                        pe.wait_ge(s["scanned"], c * NG + k + 1)
                    if held == "attn":
                        pe.wait_ge(s["x2_ready"], c + 1)
                    if held == "logits":
                        pe.wait_ge(s["lg_copied"], c + 1)
                return p_dve[turn % 2]

            def turned(bank_, tiles):
                for j in range(JT):
                    ins = pe.transpose(bank_[:, j * P:(j + 1) * P], tiles(j), ident)
                return ins

            def split_product(bank_, hi, lo, c, k, done):
                cols = slice(k * P, (k + 1) * P)
                pe.matmul(bank_[:], hi[:, cols], h2_hi[:, c % 2, :], start=True, stop=False)
                pe.matmul(bank_[:], hi[:, cols], h2_lo[:, c % 2, :], start=False, stop=False)
                pe.matmul(bank_[:], lo[:, cols], h2_hi[:, c % 2, :], start=False, stop=True).then_inc(s[done], 1)

            pe.wait_ge(s["mod_in"], 16)
            pe.wait_ge(s["act_set"], 1)
            for col, part in enumerate((0, 1, 3, 4, 2, 5)):
                ins = pe.matmul(p_out[:, col:col + 1], dense[:, M_MOD + part * D:M_MOD + (part + 1) * D], silu_c,
                                start=True, stop=True)
            ins.then_inc(s["pe_set"], 1)
            pe.wait_ge(s["const_in"], 16)
            pe.wait_ge(s["dense_in"], 16)

            for kind, c, k in pieces("pe"):
                n = c * NG + k
                piece = (kind, c, k)
                if kind == "norm1":
                    bank_ = act_bank(piece)
                    pe.wait_ge(s["xn1_ready"], JT * (c + 1))
                    turned(bank_, lambda j: xn1[:, j, :]).then_inc(s["act_full"], 1)
                if kind == "gate":
                    bank_ = act_bank(piece)
                    pe.wait_ge(s["act_free"], act_turn["norm1", c, 0] + 1)
                    pe.matmul(bank_[:], wgT, chunk(hT, c, PAD), start=True, stop=True).then_inc(s["act_full"], 1)
                if kind == "z":
                    bank_ = act_bank(piece)
                    pe.wait_ge(s["xc_ready"], c + 1)
                    pe.matmul(bank_[:], wdT, xc[:], start=True, stop=True).then_inc(s["act_full"], 1)
                if kind in ("b", "c"):
                    pe.wait_ge(s["dve_set"], 5)
                    pe.wait_ge(s["xc_ready"], c + 1)
                    pe.matmul(act_bank(piece)[:], (wb_rep if kind == "b" else wc_rep)[:], xc[:], start=True,
                              stop=True).then_inc(s["act_full"], 1)
                if kind in ("decay", "inp"):
                    g = GROUPS[k]
                    pe.wait_ge(s["picked"], 8)
                    parts, ready, bank_ = ((delta_r, "d_lo", act_bank) if kind == "decay" else
                                           (dx_r, "dx_lo", dve_bank))
                    bank_ = bank_(piece)
                    if 2 * c + 1 + g // 8 > 0:
                        pe.wait_ge(s[ready], 2 * c + 1 + g // 8)
                    pe.matmul(bank_[:], pick[:, g % 8, :], parts[:, c % 2, g // 8, :], start=True,
                              stop=True).then_inc(s["act_full" if kind == "decay" else "dve_full"], 1)
                if kind == "sum":
                    pe.wait_ge(s["hc_ready"], c * NG + QB * (k + 1))
                    if k == 0:
                        pe.wait_ge(s["proj_taken"], 2)
                        if c > 0:
                            pe.wait_ge(s["yg_ready"], c)
                    for i in range(QB):
                        ins = pe.matmul(p_y[32 * i:32 * (i + 1), :], const[:, K_SUM + 32 * k:K_SUM + 32 * (k + 1)],
                                        hc[:, (c * NG + QB * k + i) % NHC, :], start=(k == 0),
                                        stop=(k == NG // QB - 1), tile_position=(0, 32 * i))
                    ins.then_inc(s["summed"], 1)
                if kind == "attn":
                    bank_ = dve_bank(piece)
                    pe.wait_ge(s["yg_ready"], c + 1)
                    for j in range(JT):
                        ins = pe.matmul(bank_[:, j * P:(j + 1) * P], yg[:, j * P:(j + 1) * P], wo_gT[:],
                                        start=True, stop=True)
                    ins.then_inc(s["dve_full"], 1)
                if kind == "norm2":
                    bank_ = act_bank(piece)
                    pe.wait_ge(s["xn2_ready"], JT * (c + 1))
                    turned(bank_, lambda j: xn2[:, j, :]).then_inc(s["act_full"], 1)
                if kind == "logits":
                    bank_ = dve_bank(piece)
                    pe.wait_ge(s["act_free"], act_turn["norm2", c, 0] + 1)
                    for j in range(JT):
                        ins = pe.matmul(bank_[:, j * NE:(j + 1) * NE], h2[:, j * P:(j + 1) * P],
                                        small[:, C_ROUTE:C_ROUTE + NE], start=True, stop=True)
                    ins.then_inc(s["dve_full"], 1)
                if kind == "up":
                    if n == 0:
                        pe.wait_ge(s["w_lo"], 2 * NQ)
                    if k == 0:
                        pe.wait_ge(s["h2_lo_ready"], c + 1)
                    if n > 0:
                        pe.wait_ge(s["silued"], n)
                    split_product(p_gate, w0_hi, w0_lo, c, k, "gate_up")
                if kind == "lin":
                    if n > 0:
                        pe.wait_ge(s["multiplied"], n)
                    split_product(p_lin, w1_hi, w1_lo, c, k, "lin_up")
                if kind == "down":
                    expert = c * NE + k
                    pe.wait_ge(s["wo_ready"], NQ)
                    pe.wait_ge(s["multiplied"], HE * (expert + 1))
                    if expert > 0:
                        pe.wait_ge(s["part_ready"], expert)
                    for j in range(JT):
                        for i in range(HE):
                            ins = pe.matmul(p_out[:, j * P:(j + 1) * P],
                                            hid[:, (HE * expert + i) % NU, j * P:(j + 1) * P],
                                            wo[:, HE * k + i, :], start=(i == 0), stop=(i == HE - 1))
                    ins.then_inc(s["down_done"], 1)
                if kind == "proj":
                    pe.wait_ge(s["fold_ready"], 2)
                    pe.transpose(p_y[:, 0:P], wo_g[:], ident)
                    pe.matmul(p_y[:, P:2 * P], bo_g.to_broadcast([P, P]), ident, start=True, stop=True)
                    pe.matmul(p_y[:, 2 * P:3 * P], gb.to_broadcast([P, P]), ident, start=True,
                              stop=True).then_inc(s["proj_ready"], 1)


def kernel(L0_attn_x, L0_attn_conv_w, L0_attn_conv_b, L0_attn_Wd, L0_attn_bd, L0_attn_Wb, L0_attn_Wc,
           L0_attn_log_a, L0_attn_Wg, L0_attn_bg, L0_attn_Wo, L0_attn_bo, L0_ffn_gate_kernel,
           L0_ffn_w0_kernel, L0_ffn_w1_kernel, L0_ffn_wo_kernel, L0_c, L0_wmod):
    import numpy as np
    import concourse.bacc as bacc
    from concourse.bass_utils import run_bass_kernel_spmd

    def col(a):
        return np.asarray(a).reshape(D, -1)

    xa = np.asarray(L0_attn_x)
    n_tiles = xa.shape[1] // P
    loga = np.asarray(L0_attn_log_a).reshape(NG, GC, NS).transpose(2, 1, 0).reshape(P, NG)
    small = np.concatenate([col(L0_attn_conv_w), col(L0_attn_conv_b), col(L0_attn_bd), col(L0_attn_bg),
                            col(L0_attn_bo), col(L0_c), np.asarray(L0_ffn_gate_kernel), loga,
                            np.asarray(L0_attn_Wb).T, np.asarray(L0_attn_Wc).T], axis=1)
    dense = np.concatenate([np.asarray(L0_attn_Wd).T, np.asarray(L0_attn_Wg).T, np.asarray(L0_attn_Wo),
                            np.asarray(L0_wmod)], axis=1)
    const = np.zeros((P, N_CONST), np.float32)
    for p in range(P):
        const[p, K_ID + p] = 1.0
        const[p, K_FOLD + p % 64] = 1.0
        for q in range(4):
            const[p, K_SUM + 32 * q + GC * q + p % GC] = 1.0
        const[p, K_IOTA:K_IOTA + NE] = range(NE)
    arrays = {
        "x": xa.reshape(n_tiles, P, D).transpose(1, 0, 2).reshape(P, n_tiles * D),
        "small": small,
        "dense": dense,
        "const": const,
        "w0": np.asarray(L0_ffn_w0_kernel).transpose(1, 0, 2).reshape(D, NE * H),
        "w1": np.asarray(L0_ffn_w1_kernel).transpose(1, 0, 2).reshape(D, NE * H),
        "wo": np.asarray(L0_ffn_wo_kernel).reshape(NH, P, D).transpose(1, 0, 2).reshape(P, NH * D),
    }
    arrays = {k: np.ascontiguousarray(a) for k, a in arrays.items()}
    nc = bacc.Bacc("TRN2", target_bir_lowering=False, num_devices=1)
    args = [nc.dram_tensor(f"in_{k}", a.shape, F32, kind="ExternalInput").ap() for k, a in arrays.items()]
    args.append(nc.dram_tensor("out_tokens", (P, n_tiles * D), F32, kind="ExternalOutput").ap())
    program(nc, *args)
    r = run_bass_kernel_spmd(nc, [{f"in_{k}": a for k, a in arrays.items()}], core_ids=[0])
    got = r.results[0]["out_tokens"]
    return got.reshape(P, n_tiles, D).transpose(1, 0, 2).reshape(xa.shape)
```
